# Optimizing a Trainium2 kernel written in Bass

```python
import numpy as np
import jax
import jax.numpy as jnp

def _softmax(x, axis=-1):
    return jax.nn.softmax(x, axis=axis)

def _gelu(x):
    return jax.nn.gelu(x, approximate=True)

def _silu(x):
    return jax.nn.silu(x)

def _sigmoid(x):
    return jax.nn.sigmoid(x)

def _layernorm(x, axis=-1, eps=1e-05):
    m = jnp.mean(x, axis=axis, keepdims=True)
    v = jnp.var(x, axis=axis, keepdims=True)
    return (x - m) / jnp.sqrt(v + eps)

def _scatter_add(tgt, idx, src, axis=0):
    return tgt.at[idx].add(src)

def _segment_sum(src, seg, n):
    return jax.ops.segment_sum(src, seg, n)
kernel_name = 'mk_flamingo_gated_d1_seqx_r4_b667d5'

def setup_inputs(seed: int=0):
    np.random.seed(seed)
    _w = jnp.asarray

    def _rec_inputs():
        import jax
        import jax.numpy as jnp
        _rk = jax.random.key(seed)
        x = -0.0003929 + 0.9999 * jax.random.normal(jax.random.fold_in(_rk, 1), (4, 512, 256), jnp.float32)
        _lenS = 512 - jax.random.randint(jax.random.fold_in(_rk, 7), (4,), 0, max(1, 512 // 4) + 1, jnp.int32)
        _lenS2 = 1601 - jax.random.randint(jax.random.fold_in(_rk, 8), (4,), 0, max(1, 1601 // 4) + 1, jnp.int32)
        _ctx_1024P = jax.random.normal(jax.random.fold_in(_rk, 11), (4, 16, 256), jnp.float32)
        _ctx_1024c = jax.random.dirichlet(jax.random.fold_in(_rk, 511), 0.3 * jnp.ones((16,), jnp.float32), (4, 1601))
        _ctx_1024t = jnp.einsum('bsk,bkd->bsd', _ctx_1024c, _ctx_1024P)
        _ctx_1024t = _ctx_1024t * jax.lax.rsqrt(jnp.mean(jnp.square(_ctx_1024t)) + 1e-12) * 0.953939
        ctx_1024 = -0.000514642 + 1.00011 * (_ctx_1024t + 0.3 * jax.random.normal(jax.random.fold_in(_rk, 611), (4, 1601, 256), jnp.float32))
        itok_BxS_0_511 = jax.random.randint(jax.random.fold_in(_rk, 12), (4, 512), 0, 128, jnp.int32)
        _g = jax.random.normal(jax.random.fold_in(_rk, 9001), (2, 1), jnp.float32)
        _g = jnp.sign(_g) * jnp.maximum(jnp.abs(_g), 1.0) + (_g == 0) * 1.0
        g_xattn = _g[0]
        g_ffn = _g[1]
        return (x, ctx_1024, itok_BxS_0_511, g_xattn, g_ffn)
    x, ctx_1024, itok_BxS_0_511, g_xattn, g_ffn = _rec_inputs()

    def _L0_xattn_setup():
        import jax, jax.numpy as jnp
        import numpy as np
        Q_DIM = 256
        KV_DIM = 256
        D_ATTN = 256
        N_HEADS = 16
        HDIM = D_ATTN // N_HEADS
        LOOKBACK = 3
        KW = LOOKBACK + 1
        SCALE = HDIM ** (-0.5)
        B, LQ, LKV = (4, 1024, 128)

        def _split_heads(x):
            b, l, _ = x.shape
            return x.reshape(b, l, N_HEADS, HDIM).transpose(0, 2, 1, 3)
        key = jax.random.key(seed)
        ks = jax.random.split(key, 6)
        q = jax.random.normal(ks[0], (B, LQ, Q_DIM), dtype=jnp.float32)
        kv_src = jax.random.normal(ks[1], (B, LKV, KV_DIM), dtype=jnp.float32)
        seg_id = jnp.sort(jax.random.randint(ks[2], (B, LQ), 0, LKV), axis=-1)
        Wq = jax.random.normal(ks[3], (D_ATTN, Q_DIM), dtype=jnp.float32) * Q_DIM ** (-0.5)
        Wkv = jax.random.normal(ks[4], (2 * D_ATTN, KV_DIM), dtype=jnp.float32) * KV_DIM ** (-0.5)
        Wo = jax.random.normal(ks[5], (Q_DIM, D_ATTN), dtype=jnp.float32) * D_ATTN ** (-0.5)
        return {'q': q, 'kv_src': kv_src, 'seg_id': seg_id, 'Wq': Wq, 'Wkv': Wkv, 'Wo': Wo}
    _L0_xattn_all = _L0_xattn_setup()
    _L0_xattn_in = {k: v for k, v in _L0_xattn_all.items() if k in ('Wq', 'Wkv', 'Wo')}
    del _L0_xattn_all

    def _L0_ffn_setup():
        import jax, jax.numpy as jnp
        import numpy as np
        TOP_K = 2
        key = jax.random.key(seed)
        ks = jax.random.split(key, 6)
        B, S, H, F, E = (4, 512, 256, 1024, 8)
        scale = 0.02
        x = jax.random.normal(ks[0], (B, S, H), dtype=jnp.float32)
        gate_w = jax.random.normal(ks[1], (E, H), dtype=jnp.float32) * scale
        w1 = jax.random.normal(ks[2], (E, H, F), dtype=jnp.float32) * scale
        b1 = jnp.zeros((E, F), dtype=jnp.float32)
        w2 = jax.random.normal(ks[3], (E, F, H), dtype=jnp.float32) * scale
        b2 = jnp.zeros((E, H), dtype=jnp.float32)
        return {'x': x, 'gate_w': gate_w, 'w1': w1, 'b1': b1, 'w2': w2, 'b2': b2}
    _L0_ffn_all = _L0_ffn_setup()
    _L0_ffn_in = {k: v for k, v in _L0_ffn_all.items() if k in ('gate_w', 'w1', 'b1', 'w2', 'b2')}
    del _L0_ffn_all
    return {'x': x, 'ctx_1024': ctx_1024, 'itok_BxS_0_511': itok_BxS_0_511, 'g_xattn': g_xattn, 'g_ffn': g_ffn, 'L0_xattn_Wq': _L0_xattn_in['Wq'], 'L0_xattn_Wkv': _L0_xattn_in['Wkv'], 'L0_xattn_Wo': _L0_xattn_in['Wo'], 'L0_ffn_gate_w': _L0_ffn_in['gate_w'], 'L0_ffn_w1': _L0_ffn_in['w1'], 'L0_ffn_b1': _L0_ffn_in['b1'], 'L0_ffn_w2': _L0_ffn_in['w2'], 'L0_ffn_b2': _L0_ffn_in['b2']}

def reference(x, ctx_1024, itok_BxS_0_511, g_xattn, g_ffn, L0_xattn_Wq, L0_xattn_Wkv, L0_xattn_Wo, L0_ffn_gate_w, L0_ffn_w1, L0_ffn_b1, L0_ffn_w2, L0_ffn_b2):
    import jax
    import jax.numpy as jnp

    def _L0_xattn_ref(q, kv_src, seg_id, Wq, Wkv, Wo):
        import jax, jax.numpy as jnp
        import numpy as np
        Q_DIM = 256
        KV_DIM = 256
        D_ATTN = 256
        N_HEADS = 16
        HDIM = D_ATTN // N_HEADS
        LOOKBACK = 3
        KW = LOOKBACK + 1
        SCALE = HDIM ** (-0.5)
        B, LQ, LKV = (4, 1024, 128)

        def _split_heads(x):
            b, l, _ = x.shape
            return x.reshape(b, l, N_HEADS, HDIM).transpose(0, 2, 1, 3)
        b, lq, _ = q.shape
        lkv = kv_src.shape[1]
        qh = _split_heads(q @ Wq.T)
        kv = kv_src @ Wkv.T
        k, v = jnp.split(kv, 2, axis=-1)
        kh = _split_heads(k)
        vh = _split_heads(v)
        offsets = jnp.arange(KW)
        gather = seg_id[:, :, None] - offsets
        neg_mask = gather < 0
        gc = jnp.clip(gather, 0, lkv - 1)
        b_idx = jnp.arange(b)[:, None, None]
        k_sel = kh[b_idx, :, gc].transpose(0, 3, 1, 2, 4)
        v_sel = vh[b_idx, :, gc].transpose(0, 3, 1, 2, 4)
        scores = jnp.einsum('bhqd,bhqkd->bhqk', qh, k_sel) * SCALE
        neg_inf = jnp.finfo(scores.dtype).min
        scores = jnp.where(neg_mask[:, None, :, :], neg_inf, scores)
        probs = jax.nn.softmax(scores, axis=-1)
        out = jnp.einsum('bhqk,bhqkd->bhqd', probs, v_sel)
        out = out.transpose(0, 2, 1, 3).reshape(b, lq, D_ATTN)
        return out @ Wo.T

    def _L0_ffn_ref(x, gate_w, w1, b1, w2, b2):
        import jax, jax.numpy as jnp
        import numpy as np
        TOP_K = 2
        E = gate_w.shape[0]
        gate_logits = jnp.einsum('bsh,eh->bse', x, gate_w)
        gate_probs = jax.nn.softmax(gate_logits, axis=-1)
        top_v, top_i = jax.lax.top_k(gate_probs, TOP_K)
        onehot = jax.nn.one_hot(top_i, E, dtype=x.dtype)
        comb_w = jnp.einsum('bsk,bske->bse', top_v, onehot)
        out = jnp.zeros_like(x)
        for e in range(E):
            h = jax.nn.silu(jnp.einsum('bsh,hf->bsf', x, w1[e]) + b1[e])
            y = jnp.einsum('bsf,fh->bsh', h, w2[e]) + b2[e]
            out = out + y * comb_w[..., e:e + 1]
        return out
    x = x + jnp.tanh(g_xattn[0]) * _L0_xattn_ref(_layernorm(x, axis=-1), ctx_1024, itok_BxS_0_511, L0_xattn_Wq, L0_xattn_Wkv, L0_xattn_Wo)
    x = x + jnp.tanh(g_ffn[0]) * _L0_ffn_ref(_layernorm(x, axis=-1), L0_ffn_gate_w, L0_ffn_w1, L0_ffn_b1, L0_ffn_w2, L0_ffn_b2)
    return x

_drawn_inputs = setup_inputs


def setup_inputs(seed=0):
    import zlib

    import numpy as np

    out = dict(_drawn_inputs(seed))
    spreads = {'L0_ffn_b1': (0.0, 0.8), 'L0_ffn_b2': (0.0, 0.381)}
    factors = {}
    for name, (base, spread) in spreads.items():
        noise = np.random.default_rng([zlib.crc32(name.encode()), seed]).standard_normal(out[name].shape)
        drawn = base * np.exp(spread * noise) if base else spread * noise
        out[name] = jnp.asarray(drawn.astype(out[name].dtype))
    for name, factor in factors.items():
        out[name] = (out[name] * factor).astype(out[name].dtype)
    return out
```

```python
from contextlib import ExitStack

import concourse.bass as bass
from concourse import mybir

P = 128
F32 = mybir.dt.float32
F16 = mybir.dt.float16
BF16 = mybir.dt.bfloat16
I32 = mybir.dt.int32
U32 = mybir.dt.uint32
ALU = mybir.AluOpType
ACT = mybir.ActivationFunctionType
AX_X = mybir.AxisListType.X

HEADS, WIN, TOP_K = 16, 4, 2
EPS = 1e-5
MASKED = -3.0e38
X_SCALE, W_SCALE, H_SCALE = 64.0, 64.0, 4.0


def flamingo_layer(nc, x, ctx_in, seg, g_xattn, g_ffn, Wq, Wkv, Wo, gate_w, w1, b1, w2, b2, out):
    B, S, D = x.shape
    CTX = ctx_in.shape[1]
    E, _, F = w1.shape
    T = B * S // P
    TPB = S // P
    HD = D // HEADS
    KC = D // P
    FC = F // P
    NT = T * TOP_K + E - 1
    N_TOK = B * S
    CHUNKS = CTX // P
    UNITS = 4 * E
    UC = KC * F // 2
    assert TPB == 4 and KC == 2 and FC == 8 and T == 16 and UNITS == 2 * T and D == 256

    xd = nc.dram_tensor("tokens_split", (N_TOK + P, 2 * D), F16).ap()
    acc = nc.dram_tensor("rows_sum", (N_TOK + P, D), F32).ap()
    kvd = nc.dram_tensor("keys_values", (B * CTX, 2 * D), F32).ap()

    x_v = x.rearrange("b (t p) d -> p (b t) d", p=P)
    seg_row = seg.rearrange("b s -> (b s)").rearrange("(o n) -> o n", o=1)
    seg_tiles = seg.rearrange("b (t p) -> (b t) p", p=P)
    ctx_rows = ctx_in.rearrange("b s d -> (b s) d")
    ctx_first = ctx_in[:, 0:P, :].rearrange("b p d -> p b d")
    w1_v = w1.rearrange("e (k p) f -> (e k) p f", p=P)
    w2_v = w2.rearrange("e (h c p) n -> (e h) p c n", p=P, c=4)
    xd_v = xd.rearrange("(t p) d -> t p d", p=P)
    acc_v = acc[0:N_TOK, :].rearrange("(t p) d -> p t d", p=P)
    out_rows = out.rearrange("b s d -> (b s) d")

    with ExitStack() as ctx:
        def sb(name, shape, dt):
            return ctx.enter_context(nc.sbuf_tensor(name, shape, dt))

        def sem(name):
            return ctx.enter_context(nc.semaphore(name))

        w_hi = sb("w_hi", [P, UNITS, UC], F16)
        w_lo = sb("w_lo", [P, UNITS, UC], F16)
        xs = sb("xs", [P, T, D], F32)
        stage = sb("stage", [P, 2, UC], F32)
        sel = sb("sel", [P, 2, WIN, 2 * D], F32)
        seg16 = sb("seg16", [P, N_TOK], F16)
        onehot = sb("onehot", [P, 2, WIN, P], BF16)
        kv3 = sb("kv3", [P, 3, B, 2 * D], BF16)
        WqT = sb("WqT", [P, KC, D], F32)
        WoT = sb("WoT", [P, KC, D], F32)
        gateT = sb("gateT", [P, KC, E], F32)
        b1T = sb("b1T", [P, E * FC], F32)
        b1_raw = sb("b1_raw", [E * FC, P], F32)
        gate_raw = sb("gate_raw", [E, D], F32)
        b2_sb = sb("b2_sb", [E, D], F32)
        gates = sb("gates", [P, 2], F32)
        tanh_g = sb("tanh_g", [P, 2], F32)
        xn = sb("xn", [P, D], F32)
        xnT = sb("xnT", [P, KC, P], F32)
        aT = sb("aT", [P, KC, P], F32)
        x2 = sb("x2", [P, D], F32)
        x2T = sb("x2T", [P, KC, P], F32)
        xsplit = sb("xsplit", [P, 2, 2 * D], F16)
        ident = sb("ident", [P, P], F32)
        ident16 = sb("ident16", [P, P], F16)
        before = sb("before", [P, P], F16)
        ones16 = sb("ones16", [P, P], F16)
        zeros = sb("zeros", [P, 2 * D], F16)
        iota_i = x2[:, 0:P].bitcast(I32)
        iota = sb("iota", [P, P], F32)
        part_i = sb("part_i", [P, WIN], I32)
        part = sb("part", [P, WIN], F32)
        tok_i = sb("tok_i", [P, T], I32)
        tok1 = sb("tok1", [P, T], F32)
        half = sb("half", [P, T], F32)
        segr_i = x2[0:T, P:2 * P].bitcast(I32)
        segr = xn[0:T, 0:P]
        segt = sb("segt", [P, T], F32)
        mask = sb("mask", [P, T, WIN], F32)
        win_f = sb("win_f", [P, T, WIN], F32)
        win_i = sb("win_i", [P, T, WIN], I32)
        win_col = sb("win_col", [P, WIN, 1], I32)
        seg_max = sb("seg_max", [P, 1], F32)
        general_i = sb("general_i", [P, 1], I32)
        st1 = sb("st1", [P, T, 6], F32)
        mv1 = sb("mv1", [P, T, 2], F32)
        rstd1 = sb("rstd1", [P, T], F32)
        st2 = sb("st2", [P, 6], F32)
        mv2 = sb("mv2", [P, 2, 2], F32)
        var2 = sb("var2", [P, 1], F32)
        rstd2 = sb("rstd2", [P, 2, 1], F32)
        score = sb("score", [P, 2, WIN, HEADS], F32)
        prob = sb("prob", [P, 2, WIN, HEADS], F32)
        top = sb("top", [P, HEADS], F32)
        den = sb("den", [P, HEADS], F32)
        rden = sb("rden", [P, HEADS], F32)
        logit = sb("logit", [P, T, E], F32)

        sel0 = sel[:, 0, :, :].rearrange("p j c -> p (j c)")
        sel1 = sel[:, 1, :, :].rearrange("p j c -> p (j c)")
        wq_raw = sel0[:, 0:512].rearrange("p (o c) -> p o c", o=2)
        wkv_raw = sel0[:, 512:1536].rearrange("p (o c) -> p o c", o=4)
        wo_raw = sel0[:, 1536:2048].rearrange("p (o c) -> p o c", o=2)
        ctx0 = sel1[:, 0:1024].rearrange("p (b d) -> p b d", b=B)
        WkvT = sel1[:, 1024:2048].rearrange("p (k c) -> p k c", k=KC)
        ctx_g = sel1[:, 0:256]
        ctxT_g = sel1[:, 256:512].rearrange("p (k c) -> p k c", k=KC)
        kv_g = sel1[:, 512:1024]
        seg_i = stage[:, :, :].rearrange("p a c -> p (a c)").bitcast(I32)
        kv_rest = xsplit[:, :, :].rearrange("p a c -> p (a c)").bitcast(F32)
        ctxT = [x2T, aT]

        row_hot = sel[:, :, :, :].rearrange("p a j c -> p (a j c)").rearrange("p (n r) -> p n r", r=P)
        kv_words = kv3[:, :, :, :].rearrange("p a b c -> p (a b c)").bitcast(F32)
        col_val = kv_words[:, 0:2 * T * 2 * NT].rearrange("p (n a q) -> p n a q", a=2, q=NT)
        flat_x2T = x2T[:, :, :].rearrange("p k c -> p (k c)")
        flat_aT = aT[:, :, :].rearrange("p k c -> p (k c)")
        spare = seg16[:, :].bitcast(F32)

        def over(i, *dims, spare=spare):
            names = " ".join("abc"[:len(dims)])
            n = 1
            for d in dims:
                n *= d
            return spare[:, i:i + n].rearrange(f"p ({names}) -> p {names}", **dict(zip("abc", dims)))

        r_mx = sb("r_mx", [P, T], F32)
        r_ex = over(0, T, E, spare=x2[:, :])
        r_sum = sb("r_sum", [P, T], F32)
        r_rs = sb("r_rs", [P, T], F32)
        r_p = over(128, T, E, spare=x2[:, :])
        r_m8 = over(0, T, 8)
        r_i8 = over(128, T, 8).bitcast(U32)
        r_i2 = sb("r_i2", [P, T, 2], F32)
        r_oh = over(256, 2, T, E)
        r_m16 = over(192, T, E // 2, spare=flat_x2T).rearrange("p t e -> p (t e)").bitcast(F16).rearrange("p (t e) -> p t e", t=T)
        r_tot = over(512, E, T)
        r_go = sb("r_go", [P, E, T], F32)
        r_inc = over(640, E, T)
        r_exc = over(768, E, T)
        r_ni = sb("r_ni", [P, E], I32)
        r_ti = sb("r_ti", [P, E], I32)
        r_tf = sb("r_tf", [P, E], F32)
        r_one = sb("r_one", [P, E], F32)
        r_end = sb("r_end", [P, E], F32)
        r_start = sb("r_start", [P, E], F32)
        r_base = over(896, T, E)
        r_tmp = over(0, T, E, spare=xn[:, :])
        r_slot = over(0, 2, T, spare=flat_aT)
        r_si = over(32, 2, T, spare=flat_aT).bitcast(I32)
        r_qi = over(64, 2, T, spare=flat_aT).bitcast(I32)
        r_ri = over(96, 2, T, spare=flat_aT).bitcast(I32)
        r_q = over(128, 2, T, spare=flat_aT)
        r_r = over(160, 2, T, spare=flat_aT)
        r_w = sb("r_w", [P, 2, T], F32)
        r_comb = over(128, T, E, spare=xn[:, :])
        r_combT = stage[0:E, :, :].rearrange("e a c -> e (a c)").rearrange("e (t p) -> e t p", p=P)
        pad_row = sb("pad_row", [P, 1], F32)
        l_empty = flat_x2T[:, 0 * NT:1 * NT]
        l_idx = flat_x2T[:, 1 * NT:2 * NT]
        slot_row = sb("slot_row", [P, NT], I32)
        slot_w = sb("slot_w", [P, NT], F32)
        l_cmp = over(0, NT, E, spare=kv_rest)
        l_e = flat_x2T[:, 2 * NT:3 * NT]
        tile_e = sb("tile_e", [P, NT], I32)
        gcol = sb("gcol", [P, 2, 1], I32)
        scol = sb("scol", [P, 2, 1], I32)

        sel0_16 = sel0.bitcast(F16)
        xg = [sel0_16[:, 512 * i:512 * i + 512] for i in range(2)]
        xT = [sel0_16[:, 1024 + 512 * i:1536 + 512 * i].rearrange("p (a c) -> p a c", a=4) for i in range(2)]
        y_sb = [sel0[:, 1024 + 256 * i:1280 + 256 * i] for i in range(2)]
        h32 = [sel1[:, 1024 * i:1024 * i + 1024] for i in range(2)]
        kv16 = kv_words.bitcast(F16)
        h_hi = [kv16[:, 1024 * i:1024 * i + 1024] for i in range(2)]
        h_lo = [kv16[:, 2048 + 1024 * i:3072 + 1024 * i] for i in range(2)]

        ps = ctx.enter_context(nc.psum_tensor("ps", [P, 8, 512], F32))
        ps_t = ps[:, 0, :]
        ps_q = ps[:, 1, :]
        ps_sel = ps[:, 2:6, :]
        ps_a = ps[:, 6, :]
        ps_o = ps[:, 7, :]
        ps_x16 = ps[:, 0, :].bitcast(F16)
        ps_h = [ps[:, 1:3, :].rearrange("p a c -> p (a c)"), ps[:, 3:5, :].rearrange("p a c -> p (a c)")]
        ps_y = [ps[:, 5, :], ps[:, 6, :]]

        names = """unused x_in0 x_in1 x_in2 x_in3 seg_in wraw_in small_in ctx_in w_in0 w_in1 consts cast_consts
            seg_cast seg_f segt_ps setup seg_flag gates_t ps_wT ps_small wT small_T ctxT_ps ctxT_sb
            kv_ps kv_hi kv_r kv_mid kv_done
            g_ctx g_ctxT_ps g_ctxT g_kv_ps g_kv g_stored g_col g_rows
            stats1 aggr1 var1 rstd1_ok xn_ok xnT_ps xnT_ok q_ps hot_ok sel_ps sel_ok
            kprod scored masked topped shifted exped summed inverted prob_ok v_ok aT_ps aT_ok o_ps
            x1_ok stats2 aggr2 var2_ok rstd2_ok x2_ok x2hi_ok xsplit_ok xd_out0 xd_out1 x2T_ps x2T_ok logit_ps logit_ok
            w_hi_ok w_lo_ok zero_out
            rt rt_exp rt_ps list_ps combT_ps combT_ok b2_ps acc_ok acc_out
            gcol_ok scol_ok gathered0 gathered1 xT_ps xT_ok h_ps silu_ok hhi_ok hlo_ok y_ps y_ok scattered out_done""".split()
        s = {n: sem(n) for n in names}

        block = ctx.enter_context(nc.Block())

        def wait(eng, name, value):
            if not isinstance(value, int) or value > 0:
                eng.wait_ge(s[name], value)

        def wait_apart(eng, name, value):
            wait(eng, name, value)
            if not isinstance(value, int):
                eng.sem_inc(s["unused"], 1)

        def half_count(t, parity):
            return 8 * (t - parity) + 16

        def attention_steps(eng, step, lead, lag):
            def fixed(t):
                step(t, t % 4, lambda d: 0 <= t + d < T)
            for t in range(-lead, 4):
                fixed(t)
            with eng.Fori(1, 3) as b:
                for k in range(4):
                    step(b * 4 + k, k, lambda d: True)
            for t in range(12, T + lag):
                fixed(t)

        def expert_steps(eng, step, lead, lag):
            def fixed(q):
                step(q, q % 2, lambda d: 0 <= q + d < NT)
            for q in range(-lead, 2):
                fixed(q)
            with eng.Fori(1, (NT - 4) // 2) as i:
                for k in range(2):
                    step(i * 2 + k, k, lambda d: True)
            for q in range((NT - 4) // 2 * 2, NT + lag):
                fixed(q)

        def at(v):
            return slice(v, v + 1) if isinstance(v, int) else bass.ds(v, 1)

        def tile_of(ap, v):
            return ap[:, at(v), :].rearrange("p o c -> p (o c)")

        def spread_mid(ap, n):
            return ap.rearrange("p (o c) -> p o c", o=1).to_broadcast([P, n, ap.shape[1]])

        def flag(eng):
            eng.wait_ge(s["seg_flag"], 1)
            return eng.value_load(general_i[0:1, 0:1], min_val=0, max_val=1)

        @block.sync
        def _(sp):
            sp.dma_start(segr_i[:, :], seg_tiles).then_inc(s["seg_in"], 16)
            sp.dma_start(seg_i, seg_row.to_broadcast([P, N_TOK])).then_inc(s["seg_in"], 16)
            sp.dma_start(wq_raw, Wq.rearrange("(o p) c -> p o c", p=P)).then_inc(s["wraw_in"], 16)
            sp.dma_start(wkv_raw, Wkv.rearrange("(o p) c -> p o c", p=P)).then_inc(s["wraw_in"], 16)
            sp.dma_start(wo_raw, Wo.rearrange("(o p) c -> p o c", p=P)).then_inc(s["wraw_in"], 16)
            sp.dma_start(ctx0, ctx_first).then_inc(s["ctx_in"], 16)
            sp.wait_ge(s["consts"], 6)
            sp.dma_start(xd[N_TOK:N_TOK + P, :], zeros[:, :]).then_inc(s["zero_out"], 16)
            sp.dma_start(acc[N_TOK:N_TOK + P, :], zeros[:, :].bitcast(F32)).then_inc(s["zero_out"], 16)

            def chunk(n, row):
                sp.dma_start(ctx_g, ctx_rows[bass.ds(row, P), :]).then_inc(s["g_ctx"], 16)
                sp.wait_ge(s["g_kv"], n + 1)
                sp.dma_start(kvd[bass.ds(row, P), :], kv_g).then_inc(s["g_stored"], 16)
                wait_apart(sp, "g_stored", n * 16 + 16)

            general = flag(sp)
            with sp.If(general > 0):
                sp.wait_ge(s["kv_done"], B)
                with sp.Fori(0, B) as b:
                    with sp.Fori(0, CHUNKS) as c:
                        chunk(b * (CHUNKS + 1) + c, b * CTX + c * P)
                    chunk(b * (CHUNKS + 1) + CHUNKS, b * CTX + (CTX - P))

            def step(t, k, live):
                for h in range(2):
                    if live(0):
                        u = t * 2 + h
                        wait_apart(sp, "w_lo_ok", u - 1)
                        if isinstance(t, int) and t == 0 and h == 0:
                            sp.wait_ge(s["seg_cast"], 1)
                        src = (w1_v if k % 2 == 0 else w2_v)
                        e = t // 2 * 2 + h if isinstance(t, int) else (t - k) + (k // 2 * 2 + h)
                        if k % 2 == 0:
                            src = w1_v[at(e), :, :].rearrange("o p f -> p (o f)")
                            dst = stage[:, h, :]
                        else:
                            src = w2_v[at(e), :, :, :].rearrange("o p c n -> p (o c) n")
                            dst = stage[:, h, :].rearrange("p (c n) -> p c n", c=4)
                        sp.dma_start(dst, src).then_inc(s[f"w_in{h}"], 16)
                if live(-3):
                    wait_apart(sp, "xsplit_ok", t - 2)
                    sp.dma_start(xd_v[at(t - 3), :, :].rearrange("o p d -> p (o d)"),
                                 xsplit[:, (k + 1) % 2, :]).then_inc(s[f"xd_out{(k + 1) % 2}"], 16)

            attention_steps(sp, step, 0, 3)

            for b in range(B):
                sp.wait_ge(s["acc_ok"], TPB * (b + 1))
                sp.dma_start(acc_v[:, TPB * b:TPB * b + TPB, :],
                             xs[:, TPB * b:TPB * b + TPB, :]).then_inc(s["acc_out"], 16)
            sp.wait_ge(s["scattered"], 16 * NT)
            sp.dma_start(out_rows, acc[0:N_TOK, :]).then_inc(s["out_done"], 16)
            sp.wait_ge(s["out_done"], 16)
            for n in range(2):
                sp.wait_ge(s[f"xd_out{n}"], 16 * T // 2)
            sp.wait_ge(s["zero_out"], 32)

        @block.gpsimd
        def _(pool):
            pool.memset(ident[:, :], 0.0).then_inc(s["consts"], 1)
            pool.memset(before[:, :], 1.0).then_inc(s["consts"], 1)
            pool.memset(ones16[:, :], 1.0).then_inc(s["consts"], 1)
            pool.memset(half[:, :], -0.5).then_inc(s["consts"], 1)
            pool.memset(r_one[:, :], 1.0).then_inc(s["consts"], 1)
            pool.memset(zeros[:, :], 0.0).then_inc(s["consts"], 1)
            pool.memset(r_go[:, :, :], 1.0).then_inc(s["consts"], 1)
            pool.wait_ge(s["consts"], 7)
            pool.affine_select(out=ident[:, :], in_=ident[:, :], compare_op=ALU.not_equal, fill=1.0, base=0,
                               pattern=[[-1, P]], channel_multiplier=1).then_inc(s["consts"], 1)
            pool.affine_select(out=before[:, :], in_=before[:, :], compare_op=ALU.is_gt, fill=0.0, base=0,
                               pattern=[[1, P]], channel_multiplier=-1).then_inc(s["consts"], 1)
            pool.memset(r_go[:, :, 0:1], 0.0).then_inc(s["consts"], 1)
            pool.iota(iota_i[:, :], pattern=[[1, P]], base=0, channel_multiplier=0).then_inc(s["consts"], 1)
            pool.iota(part_i[:, :], pattern=[[1, WIN]], base=0, channel_multiplier=1).then_inc(s["consts"], 1)
            pool.iota(tok_i[:, :], pattern=[[P, T]], base=1, channel_multiplier=1).then_inc(s["consts"], 1)
            for b in range(B):
                pool.dma_start(xs[:, TPB * b:TPB * b + TPB, :], x_v[:, TPB * b:TPB * b + TPB, :])\
                    .then_inc(s[f"x_in{b}"], 16)
            pool.wait_ge(s["aggr1"], T)
            pool.tensor_scalar(rstd1[:, :], mv1[:, :, 1], EPS, None, ALU.add).then_inc(s["var1"], 1)
            pool.wait_ge(s["var1"], 1)
            pool.tensor_tensor(rstd1[:, :], rstd1[:, :], half[:, :], ALU.pow).then_inc(s["rstd1_ok"], 1)

            general = flag(pool)

            def step(t, k, live):
                if live(1):
                    with pool.If(general > 0):
                        pool.wait_ge(s["g_stored"], 16 * B * (CHUNKS + 1))
                        pool.wait_ge(s["setup"], 1)
                        wait(pool, "aT_ps", t)
                        for j in range(WIN):
                            pool.tensor_copy(win_col[:, j, :], win_i[:, at(t + 1), j]).then_inc(s["g_col"], 1)
                        wait_apart(pool, "g_col", t * WIN + 2 * WIN)
                        for j in range(WIN):
                            pool.indirect_dma_start(sel[:, (k + 1) % 2, j, :], None, kvd,
                                                    bass.IndirectOffsetOnAxis(win_col[:, j, :], 0))\
                                .then_inc(s["g_rows"], 16)
                        pool.wait_ge(s["g_rows"], t * 16 * WIN + 32 * WIN)
                        for j in range(WIN):
                            pool.sem_inc(s["sel_ok"], 1)
                if live(-2):
                    wait_apart(pool, "aggr2", t - 1)
                    pool.tensor_scalar(var2[:, :], mv2[:, k % 2, 1:2], EPS, None, ALU.add).then_inc(s["var2_ok"], 1)
                    pool.wait_ge(s["var2_ok"], t - 1)
                    pool.tensor_tensor(rstd2[:, k % 2, :], var2[:, :], half[:, 0:1], ALU.pow)\
                        .then_inc(s["rstd2_ok"], 1)
                if live(0):
                    pool.wait_ge(s["prob_ok"], t + 1)
                    v = sel[:, k % 2, :, D:2 * D].rearrange("p j (h d) -> p j h d", d=HD)
                    pr = prob[:, k % 2, :, :].rearrange("p j (h o) -> p j h o", o=1).to_broadcast([P, WIN, HEADS, HD])
                    pool.tensor_tensor(v, v, pr, ALU.mult).then_inc(s["v_ok"], 1)

            attention_steps(pool, step, 1, 2)

            for n in range(2):
                pool.wait_ge(s[f"xd_out{n}"], 16 * T // 2)
            pool.wait_ge(s["zero_out"], 32)
            pool.wait_ge(s["rt"], RT_LIST)

            def moe(q, k, live):
                if live(3):
                    n = (k + 1) % 2
                    wait(pool, f"gathered{n}", half_count(q + 1, n))
                    pool.tensor_copy(gcol[:, n, :], slot_row[:, at(q + 3)]).then_inc(s["gcol_ok"], 1)
                    wait(pool, "gcol_ok", q + 4)
                    wait_apart(pool, "xT_ps", q + 2)
                    pool.indirect_dma_start(xg[n], None, xd, bass.IndirectOffsetOnAxis(gcol[:, n, :], 0))\
                        .then_inc(s[f"gathered{n}"], 16)
                if live(-1):
                    n = (k + 1) % 2
                    if isinstance(q, int) and q == 1:
                        pool.wait_ge(s["acc_out"], 16 * B)
                    wait(pool, "scattered", q * 16 - 16)
                    pool.tensor_copy(scol[:, n, :], slot_row[:, at(q - 1)]).then_inc(s["scol_ok"], 1)
                    wait(pool, "scol_ok", q)
                    wait_apart(pool, "y_ok", q)
                    pool.indirect_dma_start(acc, bass.IndirectOffsetOnAxis(scol[:, n, :], 0), y_sb[n], None,
                                            compute_op=ALU.add).then_inc(s["scattered"], 16)

            expert_steps(pool, moe, 3, 1)
            pool.wait_ge(s["scattered"], 16 * NT)

        @block.scalar
        def _(act):
            act.dma_start(gates[:, 0:1], g_xattn.rearrange("(o n) -> o n", o=1).to_broadcast([P, 1]))\
                .then_inc(s["small_in"], 16)
            act.dma_start(gates[:, 1:2], g_ffn.rearrange("(o n) -> o n", o=1).to_broadcast([P, 1]))\
                .then_inc(s["small_in"], 16)
            act.dma_start(b1_raw[:, :], b1.rearrange("e (c p) -> (e c) p", p=P)).then_inc(s["small_in"], 16)
            act.dma_start(gate_raw[:, :], gate_w).then_inc(s["small_in"], 16)
            act.dma_start(b2_sb[:, :], b2).then_inc(s["small_in"], 16)
            act.wait_ge(s["small_in"], 80)
            act.activation(tanh_g[:, :], gates[:, :], ACT.Tanh).then_inc(s["gates_t"], 1)
            act.wait_ge(s["ps_wT"], 1)
            act.activation(WqT[:, :, :].rearrange("p k c -> p (k c)"), ps_sel[:, 0, :], ACT.Copy).then_inc(s["wT"], 1)
            act.activation(WkvT[:, 0, :], ps_sel[:, 1, :], ACT.Copy).then_inc(s["wT"], 1)
            act.activation(WkvT[:, 1, :], ps_sel[:, 2, :], ACT.Copy).then_inc(s["wT"], 1)
            act.activation(WoT[:, :, :].rearrange("p k c -> p (k c)"), ps_sel[:, 3, :], ACT.Copy).then_inc(s["wT"], 1)
            act.wait_ge(s["ps_small"], 1)
            act.activation(gateT[:, :, :].rearrange("p k c -> p (k c)"), ps_a[:, 0:KC * E], ACT.Copy)\
                .then_inc(s["small_T"], 1)
            act.activation(b1T[:, :], ps_a[:, 64:64 + E * FC], ACT.Copy).then_inc(s["small_T"], 1)
            for b in range(B):
                act.wait_ge(s["ctxT_ps"], b + 1)
                act.activation(ctxT[b % 2][:, :, :].rearrange("p k c -> p (k c)"),
                               ps[:, b % 2, 0:256], ACT.Copy).then_inc(s["ctxT_sb"], 1)
                act.wait_ge(s["kv_ps"], b + 1)
                act.activation(kv3[:, 0, b, :], ps_o, ACT.Copy).then_inc(s["kv_hi"], 1)
                act.wait_ge(s["kv_r"], b + 1)
                act.activation(kv3[:, 1, b, :], kv_rest, ACT.Copy).then_inc(s["kv_mid"], 1)

            general = flag(act)

            def chunk(n):
                act.wait_ge(s["g_ctxT_ps"], n + 1)
                act.activation(ctxT_g.rearrange("p k c -> p (k c)"), ps_t[:, 0:256], ACT.Copy).then_inc(s["g_ctxT"], 1)
                act.wait_ge(s["g_kv_ps"], n + 1)
                act.activation(kv_g, ps_sel[:, 0, :], ACT.Copy).then_inc(s["g_kv"], 1)

            with act.If(general > 0):
                with act.Fori(0, B * (CHUNKS + 1)) as n:
                    chunk(n)

            def step(t, k, live):
                if live(0):
                    act.wait_ge(s["shifted"], t + 1)
                    act.activation(prob[:, k % 2, :, :].rearrange("p j h -> p (j h)"),
                                   score[:, k % 2, :, :].rearrange("p j h -> p (j h)"), ACT.Exp,
                                   scale=float(HD) ** -0.5).then_inc(s["exped"], 1)
                if live(1):
                    act.wait_ge(s["xnT_ps"], t + 2)
                    wait(act, "q_ps", t + 1)
                    act.activation(xnT[:, :, :].rearrange("p k c -> p (k c)"), ps_t[:, 0:256], ACT.Copy)\
                        .then_inc(s["xnT_ok"], 1)
                    with act.If(general < 1):
                        wait(act, "aT_ps", t)
                        for j in range(WIN):
                            act.wait_ge(s["sel_ps"], t * WIN + (WIN + j + 1))
                            act.activation(sel[:, (k + 1) % 2, j, :], ps_sel[:, j, :], ACT.Copy)\
                                .then_inc(s["sel_ok"], 1)
                if live(0):
                    for h in range(2):
                        act.wait_ge(s[f"w_in{h}"], t * 16 + 16)
                        act.activation(tile_of(w_hi, t * 2 + h), stage[:, h, :], ACT.Copy, scale=W_SCALE)\
                            .then_inc(s["w_hi_ok"], 1)
                if live(-1):
                    act.wait_ge(s["aT_ps"], t)
                    wait(act, "o_ps", t - 1)
                    act.activation(aT[:, :, :].rearrange("p k c -> p (k c)"), ps_a[:, 0:256], ACT.Copy)\
                        .then_inc(s["aT_ok"], 1)
                if live(-3):
                    act.wait_ge(s["x2T_ps"], t - 2)
                    wait(act, "logit_ps", t - 3)
                    act.activation(x2T[:, :, :].rearrange("p k c -> p (k c)"), ps_t[:, 256:512], ACT.Copy)\
                        .then_inc(s["x2T_ok"], 1)
                    act.wait_ge(s["logit_ps"], t - 2)
                    act.activation(tile_of(logit, t - 3), ps_a[:, 256:256 + E], ACT.Copy).then_inc(s["logit_ok"], 1)

            attention_steps(act, step, 1, 3)

            act.wait_ge(s["rt"], RT_SHIFT)
            act.activation(r_ex[:, :, :], r_tmp[:, :, :], ACT.Exp).then_inc(s["rt_exp"], 1)
            for g in range(4):
                act.wait_ge(s["combT_ps"], g + 1)
                act.activation(r_combT[:, 4 * g:4 * g + 4, :].rearrange("e t p -> e (t p)"), ps_sel[0:E, g, :],
                               ACT.Copy).then_inc(s["combT_ok"], 1)

            def moe(q, k, live):
                if live(0):
                    e = act.value_load(tile_e[0:1, at(q)], min_val=0, max_val=E - 1)
                    wait(act, "hlo_ok", q * 2 - 2)
                    for c in range(FC):
                        if c % 4 == 0:
                            act.wait_ge(s["h_ps"], q * 2 + (c // 4 + 1))
                        act.activation(h32[k][:, c * P:c * P + P], ps_h[k][:, c * P:c * P + P], ACT.Silu,
                                       bias=b1T[:, bass.ds(e * FC + c, 1)], scale=1.0 / (X_SCALE * W_SCALE))\
                            .then_inc(s["silu_ok"], 1)

            act.wait_ge(s["rt"], RT_LIST)
            expert_steps(act, moe, 0, 0)

        @block.tensor
        def _(pe):
            pe.wait_ge(s["consts"], 8)
            pe.wait_ge(s["wraw_in"], 48)
            for o in range(2):
                for c in range(KC):
                    pe.transpose(ps_sel[:, 0, c * D + o * P:c * D + o * P + P], wq_raw[:, o, c * P:c * P + P], ident[:, :])
                    pe.transpose(ps_sel[:, 3, c * D + o * P:c * D + o * P + P], wo_raw[:, o, c * P:c * P + P], ident[:, :])
            for o in range(4):
                for c in range(KC):
                    mm = pe.transpose(ps_sel[:, 1 + c, o * P:o * P + P], wkv_raw[:, o, c * P:c * P + P], ident[:, :])
            mm.then_inc(s["ps_wT"], 1)
            pe.wait_ge(s["small_in"], 80)
            for c in range(KC):
                pe.transpose(ps_a[:, c * E:c * E + E], gate_raw[:, c * P:c * P + P], ident[0:E, 0:E])
            pe.transpose(ps_a[:, 64:64 + E * FC], b1_raw[:, :], ident[0:E * FC, 0:E * FC]).then_inc(s["ps_small"], 1)
            pe.wait_ge(s["seg_f"], 1)
            pe.wait_ge(s["wT"], 4)
            pe.transpose(ps_sel[:, 3, 0:T], segr[:, :], ident[0:T, 0:T]).then_inc(s["segt_ps"], 1)
            pe.wait_ge(s["ctx_in"], 16)
            for b in range(B):
                wait(pe, "ctxT_sb", b - 1)
                for c in range(KC):
                    mm = pe.transpose(ps[:, b % 2, P * c:P * c + P],
                                      ctx0[:, b, c * P:c * P + P], ident[:, :])
                mm.then_inc(s["ctxT_ps"], 1)
                pe.wait_ge(s["ctxT_sb"], b + 1)
                wait(pe, "kv_r", b)
                for c in range(KC):
                    mm = pe.matmul(ps_o, ctxT[b % 2][:, c, :], WkvT[:, c, :], start=(c == 0), stop=(c == KC - 1))
                mm.then_inc(s["kv_ps"], 1)

            general = flag(pe)

            def chunk(n):
                pe.wait_ge(s["g_ctx"], n * 16 + 16)
                for c in range(KC):
                    mm = pe.transpose(ps_t[:, P * c:P * c + P], ctx_g[:, c * P:c * P + P], ident[:, :])
                mm.then_inc(s["g_ctxT_ps"], 1)
                pe.wait_ge(s["g_ctxT"], n + 1)
                for c in range(KC):
                    mm = pe.matmul(ps_sel[:, 0, :], ctxT_g[:, c, :], WkvT[:, c, :], start=(c == 0), stop=(c == KC - 1))
                mm.then_inc(s["g_kv_ps"], 1)

            with pe.If(general > 0):
                with pe.Fori(0, B * (CHUNKS + 1)) as n:
                    chunk(n)

            pe.wait_ge(s["kv_done"], B)
            pe.wait_ge(s["setup"], 1)

            def step(t, k, live):
                if live(1):
                    b = (t + 1) // TPB if isinstance(t, int) else None
                    pe.wait_ge(s["xn_ok"], t + 2)
                    wait(pe, "xnT_ok", t + 1)
                    for c in range(KC):
                        mm = pe.transpose(ps_t[:, c * P:c * P + P], xn[:, c * P:c * P + P], ident[:, :])
                    mm.then_inc(s["xnT_ps"], 1)
                    with pe.If(general < 1):
                        pe.wait_ge(s["hot_ok"], t + 2)
                        for j in range(WIN):
                            wait(pe, "sel_ok", t * WIN + (j + 1))
                            for m in range(3):
                                if isinstance(t, int):
                                    rows = kv3[:, m, b, :]
                                else:
                                    rows = kv3[:, m, bass.ds(pe_batch[0] + (1 if k == 3 else 0), 1), :]\
                                        .rearrange("p o c -> p (o c)")
                                mm = pe.matmul(ps_sel[:, j, :], onehot[:, (k + 1) % 2, j, :], rows,
                                               start=(m == 0), stop=(m == 2))
                            mm.then_inc(s["sel_ps"], 1)
                    pe.wait_ge(s["xnT_ok"], t + 2)
                    wait(pe, "kprod", t + 1)
                    for c in range(KC):
                        mm = pe.matmul(ps_q[:, 0:D], xnT[:, c, :], WqT[:, c, :], start=(c == 0), stop=(c == KC - 1))
                    mm.then_inc(s["q_ps"], 1)
                if live(-1):
                    pe.wait_ge(s["aT_ok"], t)
                    wait(pe, "x1_ok", t - 1)
                    for c in range(KC):
                        mm = pe.matmul(ps_o[:, 0:D], aT[:, c, :], WoT[:, c, :], start=(c == 0), stop=(c == KC - 1))
                    mm.then_inc(s["o_ps"], 1)
                if live(-3):
                    pe.wait_ge(s["x2_ok"], t - 2)
                    for c in range(KC):
                        mm = pe.transpose(ps_t[:, 256 + c * P:256 + c * P + P], x2[:, c * P:c * P + P], ident[:, :])
                    mm.then_inc(s["x2T_ps"], 1)
                    pe.wait_ge(s["x2T_ok"], t - 2)
                    for c in range(KC):
                        mm = pe.matmul(ps_a[:, 256:256 + E], x2T[:, c, :], gateT[:, c, :],
                                       start=(c == 0), stop=(c == KC - 1))
                    mm.then_inc(s["logit_ps"], 1)
                if live(0):
                    pe.wait_ge(s["v_ok"], t + 1)
                    wait(pe, "aT_ok", t)
                    wait(pe, "logit_ok", t - 2)
                    for c in range(KC):
                        for j in range(WIN):
                            mm = pe.matmul(ps_a[:, c * P:c * P + P], sel[:, k % 2, j, D + c * P:D + c * P + P],
                                           ident[:, :], start=(j == 0), stop=(j == WIN - 1))
                    mm.then_inc(s["aT_ps"], 1)

            pe_batch = [None]

            def attention_pe():
                def fixed(t):
                    step(t, t % 4, lambda d: 0 <= t + d < T)
                for t in range(-1, 4):
                    fixed(t)
                with pe.Fori(1, 3) as b:
                    pe_batch[0] = b
                    for k in range(4):
                        step(b * 4 + k, k, lambda d: True)
                for t in range(12, T + 3):
                    fixed(t)

            attention_pe()

            pe.wait_ge(s["rt"], RT_PAIRS)
            m16 = r_m16[:, :, :].rearrange("p t e -> p (t e)")
            pe.matmul(ps_q[:, 0:P], before[:, :], m16, start=True, stop=True)
            pe.matmul(ps_q[:, P:2 * P], ones16[:, :], m16, start=True, stop=True).then_inc(s["rt_ps"], 1)
            pe.wait_ge(s["rt"], RT_COMB)
            for t in range(T):
                mm = pe.transpose(ps_sel[0:E, t // 4, (t % 4) * P:(t % 4) * P + P], r_comb[:, t, :], ident[:, :])
                if t % 4 == 3:
                    mm.then_inc(s["combT_ps"], 1)
            pe.wait_ge(s["rt"], RT_HOT)
            for n in range(2 * T):
                mm = pe.matmul(ps_o[:, 0:2 * NT], row_hot[:, n, :],
                               col_val[:, n, :, :].rearrange("p a q -> p (a q)"),
                               start=(n == 0), stop=(n == 2 * T - 1))
            mm.then_inc(s["list_ps"], 1)
            pe.wait_ge(s["combT_ok"], 4)
            for t in range(T):
                bank = ps_a if t % 2 == 0 else ps_t
                wait(pe, "acc_ok", t - 1)
                pe.matmul(bank[:, 0:D], r_combT[:, t, :], b2_sb[:, :], start=True, stop=True).then_inc(s["b2_ps"], 1)

            pe.wait_ge(s["w_lo_ok"], UNITS)
            pe.wait_ge(s["acc_ok"], T)

            def moe(q, k, live):
                if live(1):
                    n = (k + 1) % 2
                    e = pe.value_load(tile_e[0:1, at(q + 1)], min_val=0, max_val=E - 1)
                    pe.wait_ge(s["xT_ok"], q + 2)
                    wait(pe, "silu_ok", q * FC)
                    for c in range(FC):
                        products = []
                        for kc in range(KC):
                            u = bass.ds(e * 4 + kc, 1)
                            hi = w_hi[:, u, c * P:c * P + P].rearrange("p o c -> p (o c)")
                            lo = w_lo[:, u, c * P:c * P + P].rearrange("p o c -> p (o c)")
                            products += [(hi, xT[n][:, kc, :]), (hi, xT[n][:, KC + kc, :]), (lo, xT[n][:, kc, :])]
                        for i, (w, xx) in enumerate(products):
                            mm = pe.matmul(ps_h[n][:, c * P:c * P + P], w, xx, start=(i == 0),
                                           stop=(i == len(products) - 1))
                        if c % 4 == 3:
                            mm.then_inc(s["h_ps"], 1)
                if live(2):
                    wait(pe, f"gathered{k}", half_count(q + 2, k))
                    wait(pe, "xT_ok", q + 2)
                    for c in range(4):
                        mm = pe.transpose(ps_x16[:, c * P:c * P + P], xg[k][:, c * P:c * P + P], ident16[:, :])
                    mm.then_inc(s["xT_ps"], 1)
                if live(0):
                    e = pe.value_load(tile_e[0:1, at(q)], min_val=0, max_val=E - 1)
                    wait(pe, "y_ok", q - 1)
                    for c in range(FC):
                        if c % 4 == 0:
                            pe.wait_ge(s["hlo_ok"], q * 2 + (c // 4 + 1))
                        u = bass.ds(e * 4 + (2 + c // 4), 1)
                        rhi = w_hi[:, u, (c % 4) * D:(c % 4) * D + D].rearrange("p o c -> p (o c)")
                        rlo = w_lo[:, u, (c % 4) * D:(c % 4) * D + D].rearrange("p o c -> p (o c)")
                        hi, lo = h_hi[k][:, c * P:c * P + P], h_lo[k][:, c * P:c * P + P]
                        pe.matmul(ps_y[k][:, 0:D], hi, rhi, start=(c == 0), stop=False)
                        pe.matmul(ps_y[k][:, 0:D], hi, rlo, start=False, stop=False)
                        mm = pe.matmul(ps_y[k][:, 0:D], lo, rhi, start=False, stop=(c == FC - 1))
                    mm.then_inc(s["y_ps"], 1)

            expert_steps(pe, moe, 2, 0)

        @block.vector
        def _(dve):
            v = nc.vector
            dve.wait_ge(s["consts"], 13)
            v.tensor_copy(ident16[:, :], ident[:, :]).then_inc(s["cast_consts"], 1)
            v.tensor_copy(iota[:, :], iota_i[:, :]).then_inc(s["cast_consts"], 1)
            v.tensor_copy(part[:, :], part_i[:, :]).then_inc(s["cast_consts"], 1)
            v.tensor_copy(tok1[:, :], tok_i[:, :]).then_inc(s["cast_consts"], 1)
            dve.wait_ge(s["cast_consts"], 4)
            v.tensor_scalar(pad_row[:, :], part[:, 0:1], float(N_TOK + 1), None, ALU.add).then_inc(s["cast_consts"], 1)
            dve.wait_ge(s["seg_in"], 32)
            v.tensor_copy(segr[:, :], segr_i[:, :]).then_inc(s["seg_f"], 1)
            v.tensor_scalar(seg16[:, :], seg_i, 2047.0, -8.0, ALU.min, ALU.max).then_inc(s["seg_cast"], 1)
            dve.wait_ge(s["seg_cast"], 1)
            v.tensor_reduce(seg_max[:, :], seg16[:, :], AX_X, ALU.max).then_inc(s["seg_cast"], 1)
            dve.wait_ge(s["seg_cast"], 2)
            v.tensor_scalar(general_i[:, :], seg_max[:, :], float(P), None, ALU.is_ge).then_inc(s["seg_flag"], 1)
            dve.wait_ge(s["segt_ps"], 1)
            v.tensor_copy(segt[:, :], ps_sel[:, 3, 0:T]).then_inc(s["seg_cast"], 1)
            dve.wait_ge(s["seg_cast"], 3)
            for j in range(WIN):
                v.tensor_scalar(mask[:, :, j], segt[:, :], float(j), MASKED, ALU.is_lt, ALU.mult)
                v.tensor_scalar(win_f[:, :, j], segt[:, :], float(-j), 0.0, ALU.add, ALU.max).then_inc(s["seg_cast"], 1)
            dve.wait_ge(s["seg_cast"], 3 + WIN)
            for b in range(B):
                last = v.tensor_scalar(win_i[:, TPB * b:TPB * b + TPB, :], win_f[:, TPB * b:TPB * b + TPB, :],
                                       float(CTX - 1), float(b * CTX), ALU.min, ALU.add)
            last.then_inc(s["setup"], 1)

            for b in range(B):
                dve.wait_ge(s["kv_hi"], b + 1)
                v.tensor_tensor(kv_rest, ps_o, kv3[:, 0, b, :], ALU.subtract).then_inc(s["kv_r"], 1)
                dve.wait_ge(s["kv_mid"], b + 1)
                v.tensor_tensor(kv3[:, 2, b, :], kv_rest, kv3[:, 1, b, :], ALU.subtract).then_inc(s["kv_done"], 1)
                if b < B - 1:
                    dve.wait_ge(s["kv_done"], b + 1)

            for b in range(B):
                dve.wait_ge(s[f"x_in{b}"], 16)
                for t in range(TPB * b, TPB * b + TPB):
                    v.bn_stats(st1[:, t, :], xs[:, t, :]).then_inc(s["stats1"], 1)
            for t in range(T):
                dve.wait_ge(s["stats1"], t + 1)
                v.bn_aggr(mv1[:, t, :], st1[:, t, :]).then_inc(s["aggr1"], 1)
            dve.wait_ge(s["rstd1_ok"], 1)
            dve.wait_ge(s["gates_t"], 1)

            general = flag(dve)

            def step(t, k, live):
                c, n = k % 2, (k + 1) % 2
                if live(0):
                    keys = sel[:, c, :, 0:D]
                    dve.wait_ge(s["q_ps"], t + 1)
                    dve.wait_ge(s["sel_ok"], t * WIN + WIN)
                    v.tensor_tensor(keys, keys, spread_mid(ps_q[:, 0:D], WIN), ALU.mult).then_inc(s["kprod"], 1)
                    dve.wait_ge(s["kprod"], t + 1)
                    v.tensor_reduce(score[:, c, :, :], keys.rearrange("p j (h d) -> p j h d", d=HD), AX_X, ALU.add)\
                        .then_inc(s["scored"], 1)
                    dve.wait_ge(s["scored"], t + 1)
                    m = tile_of(mask, t).rearrange("p (j o) -> p j o", o=1).to_broadcast([P, WIN, HEADS])
                    v.tensor_tensor(score[:, c, :, :], score[:, c, :, :], m, ALU.add).then_inc(s["masked"], 1)
                    dve.wait_ge(s["masked"], t + 1)
                    v.tensor_reduce(top[:, :], score[:, c, :, :].rearrange("p j h -> p h j"), AX_X, ALU.max)\
                        .then_inc(s["topped"], 1)
                    dve.wait_ge(s["topped"], t + 1)
                    v.tensor_tensor(score[:, c, :, :], score[:, c, :, :], spread_mid(top[:, :], WIN), ALU.subtract)\
                        .then_inc(s["shifted"], 1)
                if live(-2):
                    dve.wait_ge(s["o_ps"], t - 1)
                    row = tile_of(xs, t - 2)
                    v.scalar_tensor_tensor(out=row, in0=ps_o[:, 0:D], scalar=tanh_g[:, 0:1], in1=row,
                                           op0=ALU.mult, op1=ALU.add).then_inc(s["x1_ok"], 1)
                    wait_apart(dve, "x1_ok", t - 1)
                    v.bn_stats(st2[:, :], row).then_inc(s["stats2"], 1)
                    wait_apart(dve, "stats2", t - 1)
                    v.bn_aggr(mv2[:, c, :], st2[:, :]).then_inc(s["aggr2"], 1)
                if live(2):
                    with dve.If(general < 1):
                        wait(dve, "sel_ps", t * WIN + WIN)
                        for j in range(WIN):
                            if isinstance(t, int):
                                sg = seg16[:, (t + 2) * P:(t + 3) * P]
                            else:
                                sg = seg16[:, bass.ds((t + 2) * P, P)]
                            last = v.tensor_scalar(onehot[:, c, j, :], sg, float(j), part[:, j:j + 1],
                                                   ALU.max, ALU.is_equal)
                        last.then_inc(s["hot_ok"], 1)
                    wait(dve, "xnT_ps", t + 2)
                    v.tensor_scalar(xn[:, :], tile_of(xs, t + 2), mv1[:, at(t + 2), 0], rstd1[:, at(t + 2)],
                                    ALU.subtract, ALU.mult).then_inc(s["xn_ok"], 1)
                if live(0):
                    dve.wait_ge(s["exped"], t + 1)
                    v.tensor_reduce(den[:, :], prob[:, c, :, :].rearrange("p j h -> p h j"), AX_X, ALU.add)\
                        .then_inc(s["summed"], 1)
                    dve.wait_ge(s["summed"], t + 1)
                    v.reciprocal(rden[:, :], den[:, :]).then_inc(s["inverted"], 1)
                    dve.wait_ge(s["inverted"], t + 1)
                    v.tensor_tensor(prob[:, c, :, :], prob[:, c, :, :], spread_mid(rden[:, :], WIN), ALU.mult)\
                        .then_inc(s["prob_ok"], 1)
                if live(-2):
                    dve.wait_ge(s["rstd2_ok"], t - 1)
                    wait(dve, "x2T_ps", t - 2)
                    row = tile_of(xs, t - 2)
                    v.tensor_scalar(x2[:, :], row, mv2[:, c, 0:1], rstd2[:, c, :], ALU.subtract, ALU.mult)\
                        .then_inc(s["x2_ok"], 1)
                    dve.wait_ge(s["x2_ok"], t - 1)
                    wait(dve, f"xd_out{c}", half_count(t - 4, c))
                    v.tensor_scalar(xsplit[:, c, 0:D], x2[:, :], X_SCALE, None, ALU.mult).then_inc(s["x2hi_ok"], 1)
                    dve.wait_ge(s["x2hi_ok"], t - 1)
                    v.scalar_tensor_tensor(out=xsplit[:, c, D:2 * D], in0=x2[:, :], scalar=X_SCALE,
                                           in1=xsplit[:, c, 0:D], op0=ALU.mult, op1=ALU.subtract)\
                        .then_inc(s["xsplit_ok"], 1)
                if live(0):
                    for h in range(2):
                        dve.wait_ge(s["w_hi_ok"], t * 2 + (h + 1))
                        v.scalar_tensor_tensor(out=tile_of(w_lo, t * 2 + h), in0=stage[:, h, :], scalar=W_SCALE,
                                               in1=tile_of(w_hi, t * 2 + h), op0=ALU.mult, op1=ALU.subtract)\
                            .then_inc(s["w_lo_ok"], 1)

            attention_steps(dve, step, 2, 2)

            done = [0]

            def link(ins):
                done[0] += 1
                ins.then_inc(s["rt"], 1)
                dve.wait_ge(s["rt"], done[0])

            def by_expert(ap):
                return ap.rearrange("p (t o) -> p t o", o=1).to_broadcast([P, T, E])

            dve.wait_ge(s["logit_ok"], T)
            link(v.tensor_reduce(r_mx[:, :], logit[:, :, :], AX_X, ALU.max))
            link(v.tensor_tensor(r_tmp[:, :, :], logit[:, :, :], by_expert(r_mx[:, :]), ALU.subtract))
            assert done[0] == RT_SHIFT
            dve.wait_ge(s["rt_exp"], 1)
            link(v.tensor_reduce(r_sum[:, :], r_ex[:, :, :], AX_X, ALU.add))
            link(v.reciprocal(r_rs[:, :], r_sum[:, :]))
            link(v.tensor_tensor(r_p[:, :, :], r_ex[:, :, :], by_expert(r_rs[:, :]), ALU.mult))
            for t in range(T):
                ins = v.max(r_m8[:, t, :], r_p[:, t, :])
            link(ins)
            for t in range(T):
                ins = v.max_index(r_i8[:, t, :], r_m8[:, t, :], r_p[:, t, :])
            link(ins)
            link(v.tensor_copy(r_i2[:, :, :], r_i8[:, :, 0:2]))
            experts = spread_mid(iota[:, 0:E], T)
            for a in range(2):
                ins = v.tensor_tensor(r_oh[:, a, :, :], r_i2[:, :, a:a + 1].to_broadcast([P, T, E]), experts,
                                      ALU.is_equal)
            link(ins)
            link(v.tensor_tensor(r_m16[:, :, :], r_oh[:, 0, :, :], r_oh[:, 1, :, :], ALU.add))
            assert done[0] == RT_PAIRS
            for a in range(2):
                ins = v.tensor_scalar(r_w[:, a, :], r_m8[:, :, a], tanh_g[:, 1:2], None, ALU.mult)
            link(ins)
            for a in range(2):
                ins = v.tensor_tensor((r_ex, r_tmp)[a][:, :, :], r_oh[:, a, :, :], by_expert(r_w[:, a, :]), ALU.mult)
            link(ins)
            link(v.tensor_tensor(r_comb[:, :, :], r_ex[:, :, :], r_tmp[:, :, :], ALU.add))
            assert done[0] == RT_COMB
            dve.wait_ge(s["rt_ps"], 1)
            totals = ps_q[:, P:2 * P].rearrange("p (t e) -> p e t", e=E)
            link(v.tensor_copy(r_tot[:, :, :], totals))
            link(v.tensor_tensor_scan(r_inc[:, :, :].rearrange("p e t -> p (e t)"),
                                      r_go[:, :, :].rearrange("p e t -> p (e t)"),
                                      r_tot[:, :, :].rearrange("p e t -> p (e t)"), 0.0, ALU.mult, ALU.add))
            link(v.tensor_tensor(r_exc[:, :, :], r_inc[:, :, :], r_tot[:, :, :], ALU.subtract))
            link(v.tensor_scalar(r_ni[:, :], r_inc[:, :, T - 1], float(P - 1), None, ALU.add))
            link(v.tensor_scalar(r_ti[:, :], r_ni[:, :], 7, None, ALU.logical_shift_right))
            link(v.tensor_copy(r_tf[:, :], r_ti[:, :]))
            link(v.tensor_tensor_scan(r_end[:, :], r_one[:, :], r_tf[:, :], 0.0, ALU.mult, ALU.add))
            link(v.tensor_tensor(r_start[:, :], r_end[:, :], r_tf[:, :], ALU.subtract))
            link(v.tensor_scalar(r_start[:, :], r_start[:, :], float(P), None, ALU.mult))
            link(v.tensor_tensor(r_base[:, :, :], ps_q[:, 0:P].rearrange("p (t e) -> p t e", e=E),
                                 r_exc[:, :, :].rearrange("p e t -> p t e"), ALU.add))
            link(v.tensor_tensor(r_base[:, :, :], r_base[:, :, :], spread_mid(r_start[:, :], T), ALU.add))
            for a in range(2):
                link(v.tensor_tensor(r_tmp[:, :, :], r_oh[:, a, :, :], r_base[:, :, :], ALU.mult))
                link(v.tensor_reduce(r_slot[:, a, :], r_tmp[:, :, :], AX_X, ALU.add))
            link(v.tensor_copy(r_si[:, :, :], r_slot[:, :, :]))
            v.tensor_scalar(r_qi[:, :, :], r_si[:, :, :], 7, None, ALU.logical_shift_right)
            link(v.tensor_scalar(r_ri[:, :, :], r_si[:, :, :], P - 1, None, ALU.bitwise_and))
            v.tensor_copy(r_q[:, :, :], r_qi[:, :, :])
            link(v.tensor_copy(r_r[:, :, :], r_ri[:, :, :]))
            link(v.tensor_scalar(r_w[:, :, :], r_w[:, :, :], 1.0 / (H_SCALE * W_SCALE), None, ALU.mult))
            dve.wait_ge(s["aT_ps"], T)
            r_all = r_r[:, :, :].rearrange("p a t -> p (a t)").rearrange("p (n o) -> p n o", o=1)
            q_all = r_q[:, :, :].rearrange("p a t -> p (a t)").rearrange("p (n o) -> p n o", o=1)
            w_all = r_w[:, :, :].rearrange("p a t -> p (a t)").rearrange("p (n o) -> p n o", o=1)
            v.tensor_tensor(row_hot, spread_mid(iota[:, :], 2 * T), r_all.to_broadcast([P, 2 * T, P]), ALU.is_equal)
            link(v.tensor_tensor(col_val[:, :, 0, :], spread_mid(iota[:, 0:NT], 2 * T),
                                 q_all.to_broadcast([P, 2 * T, NT]), ALU.is_equal))
            link(v.tensor_tensor(col_val[:, :, 1, :], col_val[:, :, 0, :], w_all.to_broadcast([P, 2 * T, NT]), ALU.mult))
            for a in range(2):
                half_val = col_val[:, T * a:T * a + T, 0, :]
                ins = v.tensor_tensor(half_val, half_val,
                                      tok1[:, :].rearrange("p (t o) -> p t o", o=1).to_broadcast([P, T, NT]), ALU.mult)
            link(ins)
            assert done[0] == RT_HOT
            tiles = iota[:, 0:NT].rearrange("p (q o) -> p q o", o=1).to_broadcast([P, NT, E])
            for n in range(2):
                dve.wait_ge(s[f"xd_out{n}"], 16 * T // 2)
            link(v.tensor_tensor(l_cmp[:, :, :], spread_mid(r_end[:, :], NT), tiles, ALU.is_le))
            link(v.tensor_reduce(l_e[:, :], l_cmp[:, :, :], AX_X, ALU.add))
            link(v.tensor_scalar(tile_e[:, :], l_e[:, :], float(E - 1), None, ALU.min))
            dve.wait_ge(s["list_ps"], 1)
            link(v.tensor_scalar(l_empty[:, :], ps_o[:, 0:NT], 0.5, pad_row[:, 0:1], ALU.is_lt, ALU.mult))
            link(v.tensor_scalar(l_idx[:, :], ps_o[:, 0:NT], -1.0, None, ALU.add))
            v.tensor_copy(slot_w[:, :], ps_o[:, NT:2 * NT])
            link(v.tensor_tensor(slot_row[:, :], l_idx[:, :], l_empty[:, :], ALU.add))
            assert done[0] == RT_LIST
            for t in range(T):
                dve.wait_ge(s["b2_ps"], t + 1)
                bank = ps_a if t % 2 == 0 else ps_t
                v.tensor_tensor(xs[:, t, :], bank[:, 0:D], xs[:, t, :], ALU.add).then_inc(s["acc_ok"], 1)

            def moe(q, k, live):
                if live(0):
                    for h in range(2):
                        cols = slice(512 * h, 512 * h + 512)
                        dve.wait_ge(s["silu_ok"], q * FC + 4 * (h + 1))
                        wait(dve, "y_ps", q - 1)
                        v.tensor_scalar(h_hi[k][:, cols], h32[k][:, cols], H_SCALE, None, ALU.mult)\
                            .then_inc(s["hhi_ok"], 1)
                        dve.wait_ge(s["hhi_ok"], q * 2 + (h + 1))
                        v.scalar_tensor_tensor(out=h_lo[k][:, cols], in0=h32[k][:, cols], scalar=H_SCALE,
                                               in1=h_hi[k][:, cols], op0=ALU.mult, op1=ALU.subtract)\
                            .then_inc(s["hlo_ok"], 1)
                if live(2):
                    dve.wait_ge(s["xT_ps"], q + 3)
                    wait(dve, "h_ps", q * 2 + 2)
                    v.tensor_copy(xT[k].rearrange("p a c -> p (a c)"), ps_x16[:, 0:512]).then_inc(s["xT_ok"], 1)
                if live(-1):
                    n = (k + 1) % 2
                    dve.wait_ge(s["y_ps"], q)
                    wait(dve, "scattered", q * 16 - 32)
                    v.tensor_scalar(y_sb[n], ps_y[n][:, 0:D], slot_w[:, at(q - 1)], None, ALU.mult)\
                        .then_inc(s["y_ok"], 1)

            expert_steps(dve, moe, 2, 1)


RT_SHIFT, RT_PAIRS, RT_COMB, RT_HOT, RT_LIST = 2, 10, 13, 35, 41

_INS = ["x", "ctx_1024", "itok_BxS_0_511", "g_xattn", "g_ffn", "L0_xattn_Wq", "L0_xattn_Wkv", "L0_xattn_Wo",
        "L0_ffn_gate_w", "L0_ffn_w1", "L0_ffn_b1", "L0_ffn_w2", "L0_ffn_b2"]


def kernel(**inputs):
    import numpy as _np
    import concourse.bacc as _bacc
    from concourse import mybir as _mybir
    from concourse.bass_utils import run_bass_kernel_spmd as _run

    nc = _bacc.Bacc("TRN2", target_bir_lowering=False, num_devices=1)
    arrays, args = {}, []
    for name in _INS:
        a = _np.ascontiguousarray(inputs[name])
        arrays[f"in_{name}"] = a
        args.append(nc.dram_tensor(f"in_{name}", a.shape, _mybir.dt.from_np(a.dtype), kind="ExternalInput").ap())
    shape = inputs["x"].shape
    args.append(nc.dram_tensor("out_0", shape, _mybir.dt.float32, kind="ExternalOutput").ap())
    flamingo_layer(nc, *args)
    r = _run(nc, [arrays], core_ids=[0])
    return r.results[0]["out_0"]
```

```python
from contextlib import ExitStack

import concourse.bass as bass
from concourse import mybir

P = 128
F32 = mybir.dt.float32
F16 = mybir.dt.float16
BF16 = mybir.dt.bfloat16
I32 = mybir.dt.int32
U8 = mybir.dt.uint8
U32 = mybir.dt.uint32
ALU = mybir.AluOpType
ACT = mybir.ActivationFunctionType
AX_X = mybir.AxisListType.X

HEADS, WIN, TOP_K = 16, 4, 2
EPS = 1e-5
MASKED = -3.0e38
X_SCALE, W_SCALE, H_SCALE = 64.0, 64.0, 4.0


def flamingo_layer(nc, x, ctx_in, seg, g_xattn, g_ffn, Wq, Wkv, Wo, gate_w, w1, b1, w2, b2, out):
    B, S, D = x.shape
    CTX = ctx_in.shape[1]
    E, _, F = w1.shape
    T = B * S // P
    TPB = S // P
    HD = D // HEADS
    KC = D // P
    FC = F // P
    NT = T * TOP_K + E - 1
    N_TOK = B * S
    CHUNKS = CTX // P
    UNITS = 4 * E
    UC = KC * F // 2
    assert TPB == 4 and KC == 2 and FC == 8 and T == 16 and UNITS == 2 * T and D == 256

    xd = nc.dram_tensor("tokens_split", (N_TOK + P, 2 * D), F16).ap()
    acc = nc.dram_tensor("rows_sum", (N_TOK + P, D), F32).ap()
    kvd = nc.dram_tensor("keys_values", (B * CTX, 2 * D), F32).ap()

    x_v = x.rearrange("b (t p) d -> p (b t) d", p=P)
    seg_row = seg.rearrange("b s -> (b s)").rearrange("(o n) -> o n", o=1)
    seg_tiles = seg.rearrange("b (t p) -> (b t) p", p=P)
    ctx_rows = ctx_in.rearrange("b s d -> (b s) d")
    ctx_first = ctx_in[:, 0:P, :].rearrange("b p d -> p b d")
    w1_v = w1.rearrange("e (k p) f -> e p k f", p=P)
    w2_v = w2.rearrange("e (c p) n -> e p c n", p=P)
    xd_v = xd.rearrange("(t p) d -> t p d", p=P)
    acc_v = acc[0:N_TOK, :].rearrange("(t p) d -> p t d", p=P)
    out_rows = out.rearrange("b s d -> (b s) d")

    with ExitStack() as ctx:
        def sb(name, shape, dt):
            return ctx.enter_context(nc.sbuf_tensor(name, shape, dt))

        def sem(name):
            return ctx.enter_context(nc.semaphore(name))

        w_parts = sb("w_parts", [P, UNITS + 2, 2, UC], F16)
        xs = sb("xs", [P, T, D], F32)
        sel = sb("sel", [P, 2, WIN, 2 * D], F32)
        seg16 = sb("seg16", [P, N_TOK], F16)
        onehot = sb("onehot", [P, 2, WIN, P], BF16)
        kv3 = sb("kv3", [P, 3, B, 2 * D], BF16)
        WqT = sb("WqT", [P, KC, D], F32)
        WoT = sb("WoT", [P, KC, D], F32)
        gateT = sb("gateT", [P, KC, E], F32)
        b1T = sb("b1T", [P, E * FC], F32)
        b1_raw = sb("b1_raw", [E * FC, P], F32)
        gate_raw = sb("gate_raw", [E, D], F32)
        b2_sb = sb("b2_sb", [E, D], F32)
        gates = sb("gates", [P, 2], F32)
        tanh_g = sb("tanh_g", [P, 2], F32)
        xn = sb("xn", [P, D], F32)
        xnT = sb("xnT", [P, KC, P], F32)
        aT = sb("aT", [P, KC, P], F32)
        x2 = sb("x2", [P, D], F32)
        x2T = sb("x2T", [P, KC, P], F32)
        xsplit = sb("xsplit", [P, 2, 2 * D], F16)
        ident = sb("ident", [P, P], F32)
        ident16 = sb("ident16", [P, P], F16)
        before = sb("before", [P, P], F16)
        ones16 = sb("ones16", [P, P], F16)
        zeros = sb("zeros", [P, 2 * D], F16)
        iota_i = x2[:, 0:P].bitcast(I32)
        iota = sb("iota", [P, P], F32)
        part_i = sb("part_i", [P, WIN], I32)
        part = sb("part", [P, WIN], F32)
        tok_i = sb("tok_i", [P, T], I32)
        tok1 = sb("tok1", [P, T], F32)
        half = sb("half", [P, T], F32)
        segr_i = x2[0:T, P:2 * P].bitcast(I32)
        segr = xn[0:T, 0:P]
        segt = sb("segt", [P, T], F32)
        mask = sb("mask", [P, T, WIN], F32)
        win_f = sb("win_f", [P, T, WIN], F32)
        win_i = sb("win_i", [P, T, WIN], I32)
        win_col = sb("win_col", [P, WIN, 1], I32)
        seg_max = sb("seg_max", [P, 1], F32)
        general_i = sb("general_i", [P, 1], I32)
        st1 = sb("st1", [P, T, 6], F32)
        mv1 = sb("mv1", [P, T, 2], F32)
        rstd1 = sb("rstd1", [P, T], F32)
        st2 = sb("st2", [P, 6], F32)
        mv2 = sb("mv2", [P, 2, 2], F32)
        var2 = sb("var2", [P, 1], F32)
        rstd2 = sb("rstd2", [P, 2, 1], F32)
        score = sb("score", [P, 2, WIN, HEADS], F32)
        prob = sb("prob", [P, 2, WIN, HEADS], F32)
        top = sb("top", [P, HEADS], F32)
        den = sb("den", [P, HEADS], F32)
        rden = sb("rden", [P, HEADS], F32)
        logit = sb("logit", [P, T, E], F32)

        sel0 = sel[:, 0, :, :].rearrange("p j c -> p (j c)")
        sel1 = sel[:, 1, :, :].rearrange("p j c -> p (j c)")
        wq_raw = sel0[:, 0:512].rearrange("p (o c) -> p o c", o=2)
        wkv_raw = sel0[:, 512:1536].rearrange("p (o c) -> p o c", o=4)
        wo_raw = sel0[:, 1536:2048].rearrange("p (o c) -> p o c", o=2)
        ctx0 = sel1[:, 0:1024].rearrange("p (b d) -> p b d", b=B)
        WkvT = sel1[:, 1024:2048].rearrange("p (k c) -> p k c", k=KC)
        ctx_g = sel1[:, 0:256]
        ctxT_g = sel1[:, 256:512].rearrange("p (k c) -> p k c", k=KC)
        kv_g = sel1[:, 512:1024]
        last_places = w_parts[:, UNITS:UNITS + 2, :, :].rearrange("p u a c -> p (u a c)")
        seg_i = last_places.bitcast(I32)
        kv_rest = xsplit[:, :, :].rearrange("p a c -> p (a c)").bitcast(F32)
        ctxT = [x2T, aT]

        row_hot = sel[:, :, :, :].rearrange("p a j c -> p (a j c)").rearrange("p (n r) -> p n r", r=P)
        kv_words = kv3[:, :, :, :].rearrange("p a b c -> p (a b c)").bitcast(F32)
        col_val = kv_words[:, 0:2 * T * 2 * NT].rearrange("p (n a q) -> p n a q", a=2, q=NT)
        flat_x2T = x2T[:, :, :].rearrange("p k c -> p (k c)")
        flat_aT = aT[:, :, :].rearrange("p k c -> p (k c)")
        spare = seg16[:, :].bitcast(F32)

        def over(i, *dims, spare=spare):
            names = " ".join("abc"[:len(dims)])
            n = 1
            for d in dims:
                n *= d
            return spare[:, i:i + n].rearrange(f"p ({names}) -> p {names}", **dict(zip("abc", dims)))

        r_mx = sb("r_mx", [P, T], F32)
        r_ex = over(0, T, E, spare=x2[:, :])
        r_sum = sb("r_sum", [P, T], F32)
        r_rs = sb("r_rs", [P, T], F32)
        r_p = over(128, T, E, spare=x2[:, :])
        r_m8 = over(0, T, 8)
        r_i8 = over(128, T, 8).bitcast(U32)
        r_i2 = sb("r_i2", [P, T, 2], F32)
        r_oh = over(256, 2, T, E)
        r_m16 = over(192, T, E // 2, spare=flat_x2T).rearrange("p t e -> p (t e)").bitcast(F16).rearrange("p (t e) -> p t e", t=T)
        r_tot = over(512, E, T)
        r_go = sb("r_go", [P, E, T], F32)
        r_inc = over(640, E, T)
        r_exc = over(768, E, T)
        r_ni = sb("r_ni", [P, E], I32)
        r_ti = sb("r_ti", [P, E], I32)
        r_tf = sb("r_tf", [P, E], F32)
        r_one = sb("r_one", [P, E], F32)
        r_end = sb("r_end", [P, E], F32)
        r_start = sb("r_start", [P, E], F32)
        r_base = over(896, T, E)
        r_tmp = over(0, T, E, spare=xn[:, :])
        r_slot = over(0, 2, T, spare=flat_aT)
        r_si = over(32, 2, T, spare=flat_aT).bitcast(I32)
        r_qi = over(64, 2, T, spare=flat_aT).bitcast(I32)
        r_ri = over(96, 2, T, spare=flat_aT).bitcast(I32)
        r_q = over(128, 2, T, spare=flat_aT)
        r_r = over(160, 2, T, spare=flat_aT)
        r_w = sb("r_w", [P, 2, T], F32)
        r_comb = over(128, T, E, spare=xn[:, :])
        r_combT = last_places[0:E, :].bitcast(F32).rearrange("e (t p) -> e t p", p=P)
        pad_row = sb("pad_row", [P, 1], F32)
        l_empty = flat_x2T[:, 0 * NT:1 * NT]
        l_idx = flat_x2T[:, 1 * NT:2 * NT]
        slot_row = sb("slot_row", [P, NT], I32)
        slot_w = sb("slot_w", [P, NT], F32)
        l_cmp = over(0, NT, E, spare=kv_rest)
        l_e = flat_x2T[:, 2 * NT:3 * NT]
        tile_e = sb("tile_e", [P, NT], I32)
        gcol = sb("gcol", [P, 2, 1], I32)
        scol = sb("scol", [P, 2, 1], I32)

        sel0_16 = sel0.bitcast(F16)
        xg = [sel0_16[:, 512 * i:512 * i + 512] for i in range(2)]
        xT = [sel0_16[:, 1024 + 512 * i:1536 + 512 * i].rearrange("p (a c) -> p a c", a=4) for i in range(2)]
        y_sb = [sel0[:, 1024 + 256 * i:1280 + 256 * i] for i in range(2)]
        h32 = [sel1[:, 1024 * i:1024 * i + 1024] for i in range(2)]
        kv16 = kv_words.bitcast(F16)
        h_hi = [kv16[:, 1024 * i:1024 * i + 1024] for i in range(2)]
        h_lo = [kv16[:, 2048 + 1024 * i:3072 + 1024 * i] for i in range(2)]

        ps = ctx.enter_context(nc.psum_tensor("ps", [P, 8, 512], F32))
        ps_t = ps[:, 0, :]
        ps_q = ps[:, 1, :]
        ps_sel = ps[:, 2:6, :]
        ps_a = ps[:, 6, :]
        ps_o = ps[:, 7, :]
        ps_x16 = ps[:, 0, :].bitcast(F16)
        ps_h = [ps[:, 1:3, :].rearrange("p a c -> p (a c)"), ps[:, 3:5, :].rearrange("p a c -> p (a c)")]
        ps_y = [ps[:, 5, :], ps[:, 6, :]]

        names = """unused x_in0 x_in1 x_in2 x_in3 seg_in wraw_in small_in ctx_in w_in0 w_in1 w_in2 w_in3 consts cast_consts
            seg_cast seg_f segt_ps setup seg_flag gates_t ps_wT ps_small wT small_T ctxT_ps ctxT_sb
            kv_ps kv_hi kv_r kv_mid kv_done
            g_ctx g_ctxT_ps g_ctxT g_kv_ps g_kv g_stored g_col g_rows
            stats1 aggr1 var1 rstd1_ok xn_ok xnT_ps xnT_ok q_ps hot_ok sel_ps sel_ok
            kprod scored masked topped shifted exped summed inverted prob_ok v_ok aT_ps aT_ok o_ps
            x1_ok stats2 aggr2 var2_ok rstd2_ok x2_ok x2hi_ok xsplit_ok xd_out0 xd_out1 x2T_ps x2T_ok logit_ps logit_ok
            w_scaled w_hi_ok0 w_hi_ok1 w_lo_ok0 w_lo_ok1 zero_out
            rt rt_exp rt_ps list_ps combT_ps combT_ok b2_ps acc_ok acc_out
            gcol_ok scol_ok gathered0 gathered1 xT_ps xT_ok h_ps silu_ok hhi_ok hlo_ok y_ps y_ok scattered out_done""".split()
        s = {n: sem(n) for n in names}

        block = ctx.enter_context(nc.Block())

        def wait(eng, name, value):
            if not isinstance(value, int) or value > 0:
                eng.wait_ge(s[name], value)

        def wait_apart(eng, name, value):
            wait(eng, name, value)
            if not isinstance(value, int):
                eng.sem_inc(s["unused"], 1)

        def half_count(t, parity):
            return 8 * (t - parity) + 16

        def attention_steps(eng, step, lead, lag):
            def fixed(t):
                step(t, t % 4, lambda d: 0 <= t + d < T)
            for t in range(-lead, 4):
                fixed(t)
            with eng.Fori(1, 3) as b:
                for k in range(4):
                    step(b * 4 + k, k, lambda d: True)
            for t in range(12, T + lag):
                fixed(t)

        def expert_steps(eng, step, lead, lag):
            def fixed(q):
                step(q, q % 2, lambda d: 0 <= q + d < NT)
            for q in range(-lead, 4):
                fixed(q)
            with eng.Fori(2, (NT - 4) // 2) as i:
                for k in range(2):
                    step(i * 2 + k, k, lambda d: True)
            for q in range((NT - 4) // 2 * 2, NT + lag):
                fixed(q)

        def at(v):
            return slice(v, v + 1) if isinstance(v, int) else bass.ds(v, 1)

        def tile_of(ap, v):
            return ap[:, at(v), :].rearrange("p o c -> p (o c)")

        def spread_mid(ap, n):
            return ap.rearrange("p (o c) -> p o c", o=1).to_broadcast([P, n, ap.shape[1]])

        def raw(u):
            return w_parts[:, at(u + 2), :, :].rearrange("p o a c -> p (o a c)").bitcast(F32)

        def part_of(u, a):
            return w_parts[:, at(u), a, :].rearrange("p o c -> p (o c)")

        def flag(eng):
            eng.wait_ge(s["seg_flag"], 1)
            return eng.value_load(general_i[0:1, 0:1], min_val=0, max_val=1)

        @block.sync
        def _(sp):
            sp.dma_start(segr_i[:, :], seg_tiles).then_inc(s["seg_in"], 16)
            sp.dma_start(seg_i, seg_row.to_broadcast([P, N_TOK])).then_inc(s["seg_in"], 16)
            sp.dma_start(wq_raw, Wq.rearrange("(o p) c -> p o c", p=P)).then_inc(s["wraw_in"], 16)
            sp.dma_start(wkv_raw, Wkv.rearrange("(o p) c -> p o c", p=P)).then_inc(s["wraw_in"], 16)
            sp.dma_start(wo_raw, Wo.rearrange("(o p) c -> p o c", p=P)).then_inc(s["wraw_in"], 16)
            sp.dma_start(ctx0, ctx_first).then_inc(s["ctx_in"], 16)
            sp.wait_ge(s["consts"], 6)
            sp.dma_start(xd[N_TOK:N_TOK + P, :], zeros[:, :]).then_inc(s["zero_out"], 16)
            sp.dma_start(acc[N_TOK:N_TOK + P, :], zeros[:, :].bitcast(F32)).then_inc(s["zero_out"], 16)

            def chunk(n, row):
                sp.dma_start(ctx_g, ctx_rows[bass.ds(row, P), :]).then_inc(s["g_ctx"], 16)
                sp.wait_ge(s["g_kv"], n + 1)
                sp.dma_start(kvd[bass.ds(row, P), :], kv_g).then_inc(s["g_stored"], 16)
                wait_apart(sp, "g_stored", n * 16 + 16)

            def weights_in(t, k):
                e = t // 2 if isinstance(t, int) else (t - k) // 2 + k // 2
                if k % 2 == 0:
                    src = w1_v[at(e), :, :, :].rearrange("o p k f -> p (o k) f")
                    shape = dict(k=KC)
                else:
                    src = w2_v[at(e), :, :, :].rearrange("o p c n -> p (o c) n")
                    shape = dict(k=FC)
                places = slice(2 * t + 2, 2 * t + 4) if isinstance(t, int) else bass.ds(t * 2 + 2, 2)
                dst = w_parts[:, places, :, :].rearrange("p u a c -> p (u a c)").bitcast(F32)\
                    .rearrange("p (k n) -> p k n", **shape)
                sp.dma_start(dst, src).then_inc(s[f"w_in{k}"], 16)

            for t in range(4):
                weights_in(t, t)

            general = flag(sp)
            with sp.If(general > 0):
                sp.wait_ge(s["kv_done"], B)
                with sp.Fori(0, B) as b:
                    with sp.Fori(0, CHUNKS) as c:
                        chunk(b * (CHUNKS + 1) + c, b * CTX + c * P)
                    chunk(b * (CHUNKS + 1) + CHUNKS, b * CTX + (CTX - P))

            sp.wait_ge(s["seg_cast"], 1)

            def step(t, k, live):
                if live(4):
                    wait_apart(sp, f"w_in{k}", (t - k) * 4 + 16)
                    weights_in(t + 4, k)
                if live(-2):
                    wait_apart(sp, "xsplit_ok", t - 1)
                    sp.dma_start(xd_v[at(t - 2), :, :].rearrange("o p d -> p (o d)"),
                                 xsplit[:, k % 2, :]).then_inc(s[f"xd_out{k % 2}"], 16)

            attention_steps(sp, step, 0, 2)

            for b in range(B):
                sp.wait_ge(s["acc_ok"], TPB * (b + 1))
                sp.dma_start(acc_v[:, TPB * b:TPB * b + TPB, :],
                             xs[:, TPB * b:TPB * b + TPB, :]).then_inc(s["acc_out"], 16)
            sp.wait_ge(s["scattered"], 16 * NT)
            sp.dma_start(out_rows, acc[0:N_TOK, :]).then_inc(s["out_done"], 16)
            sp.wait_ge(s["out_done"], 16)
            for n in range(2):
                sp.wait_ge(s[f"xd_out{n}"], 16 * T // 2)
            sp.wait_ge(s["zero_out"], 32)

        @block.gpsimd
        def _(pool):
            pool.memset(ident[:, :], 0.0).then_inc(s["consts"], 1)
            pool.memset(before[:, :], 1.0).then_inc(s["consts"], 1)
            pool.memset(ones16[:, :], 1.0).then_inc(s["consts"], 1)
            pool.memset(half[:, :], -0.5).then_inc(s["consts"], 1)
            pool.memset(r_one[:, :], 1.0).then_inc(s["consts"], 1)
            pool.memset(zeros[:, :], 0.0).then_inc(s["consts"], 1)
            pool.memset(r_go[:, :, :], 1.0).then_inc(s["consts"], 1)
            pool.wait_ge(s["consts"], 7)
            pool.affine_select(out=ident[:, :], in_=ident[:, :], compare_op=ALU.not_equal, fill=1.0, base=0,
                               pattern=[[-1, P]], channel_multiplier=1).then_inc(s["consts"], 1)
            pool.affine_select(out=before[:, :], in_=before[:, :], compare_op=ALU.is_gt, fill=0.0, base=0,
                               pattern=[[1, P]], channel_multiplier=-1).then_inc(s["consts"], 1)
            pool.memset(r_go[:, :, 0:1], 0.0).then_inc(s["consts"], 1)
            pool.iota(iota_i[:, :], pattern=[[1, P]], base=0, channel_multiplier=0).then_inc(s["consts"], 1)
            pool.iota(part_i[:, :], pattern=[[1, WIN]], base=0, channel_multiplier=1).then_inc(s["consts"], 1)
            pool.iota(tok_i[:, :], pattern=[[P, T]], base=1, channel_multiplier=1).then_inc(s["consts"], 1)
            for b in range(B):
                pool.dma_start(xs[:, TPB * b:TPB * b + TPB, :], x_v[:, TPB * b:TPB * b + TPB, :])\
                    .then_inc(s[f"x_in{b}"], 16)
            pool.wait_ge(s["aggr1"], T)
            pool.tensor_scalar(rstd1[:, :], mv1[:, :, 1], EPS, None, ALU.add).then_inc(s["var1"], 1)
            pool.wait_ge(s["var1"], 1)
            pool.tensor_tensor(rstd1[:, :], rstd1[:, :], half[:, :], ALU.pow).then_inc(s["rstd1_ok"], 1)

            general = flag(pool)

            def step(t, k, live):
                if live(1):
                    with pool.If(general > 0):
                        pool.wait_ge(s["g_stored"], 16 * B * (CHUNKS + 1))
                        pool.wait_ge(s["setup"], 1)
                        wait(pool, "aT_ps", t)
                        for j in range(WIN):
                            pool.tensor_copy(win_col[:, j, :], win_i[:, at(t + 1), j]).then_inc(s["g_col"], 1)
                        wait_apart(pool, "g_col", t * WIN + 2 * WIN)
                        for j in range(WIN):
                            pool.indirect_dma_start(sel[:, (k + 1) % 2, j, :], None, kvd,
                                                    bass.IndirectOffsetOnAxis(win_col[:, j, :], 0))\
                                .then_inc(s["g_rows"], 16)
                        pool.wait_ge(s["g_rows"], t * 16 * WIN + 32 * WIN)
                        for j in range(WIN):
                            pool.sem_inc(s["sel_ok"], 1)
                if live(0):
                    pool.wait_ge(s["w_scaled"], t + 1)
                    pool.tensor_tensor(part_of(t * 2 + 1, 1), raw(t * 2 + 1), part_of(t * 2 + 1, 0), ALU.subtract)\
                        .then_inc(s["w_lo_ok1"], 1)
                    pool.wait_ge(s["prob_ok"], t + 1)
                    v = sel[:, k % 2, :, D:2 * D].rearrange("p j (h d) -> p j h d", d=HD)
                    pr = prob[:, k % 2, :, :].rearrange("p j (h o) -> p j h o", o=1).to_broadcast([P, WIN, HEADS, HD])
                    pool.tensor_tensor(v, v, pr, ALU.mult).then_inc(s["v_ok"], 1)
                if live(-1):
                    n = (k + 1) % 2
                    wait_apart(pool, "aggr2", t)
                    pool.tensor_scalar(var2[:, :], mv2[:, n, 1:2], EPS, None, ALU.add).then_inc(s["var2_ok"], 1)
                    pool.wait_ge(s["var2_ok"], t)
                    pool.tensor_tensor(rstd2[:, n, :], var2[:, :], half[:, 0:1], ALU.pow)\
                        .then_inc(s["rstd2_ok"], 1)

            attention_steps(pool, step, 1, 1)

            for n in range(2):
                pool.wait_ge(s[f"xd_out{n}"], 16 * T // 2)
            pool.wait_ge(s["zero_out"], 32)
            pool.wait_ge(s["rt"], RT_LIST)

            def moe(q, k, live):
                if live(3):
                    n = (k + 1) % 2
                    wait(pool, f"gathered{n}", half_count(q + 1, n))
                    pool.tensor_copy(gcol[:, n, :], slot_row[:, at(q + 3)]).then_inc(s["gcol_ok"], 1)
                    wait(pool, "gcol_ok", q + 4)
                    wait_apart(pool, "xT_ps", q + 2)
                    pool.indirect_dma_start(xg[n], None, xd, bass.IndirectOffsetOnAxis(gcol[:, n, :], 0))\
                        .then_inc(s[f"gathered{n}"], 16)
                if live(-1):
                    n = (k + 1) % 2
                    if isinstance(q, int) and q == 1:
                        pool.wait_ge(s["acc_out"], 16 * B)
                    wait(pool, "scattered", q * 16 - 16)
                    pool.tensor_copy(scol[:, n, :], slot_row[:, at(q - 1)]).then_inc(s["scol_ok"], 1)
                    wait(pool, "scol_ok", q)
                    wait_apart(pool, "y_ok", q)
                    pool.indirect_dma_start(acc, bass.IndirectOffsetOnAxis(scol[:, n, :], 0), y_sb[n], None,
                                            compute_op=ALU.add).then_inc(s["scattered"], 16)

            expert_steps(pool, moe, 3, 1)
            pool.wait_ge(s["scattered"], 16 * NT)

        @block.scalar
        def _(act):
            act.dma_start(gates[:, 0:1], g_xattn.rearrange("(o n) -> o n", o=1).to_broadcast([P, 1]))\
                .then_inc(s["small_in"], 16)
            act.dma_start(gates[:, 1:2], g_ffn.rearrange("(o n) -> o n", o=1).to_broadcast([P, 1]))\
                .then_inc(s["small_in"], 16)
            act.dma_start(b1_raw[:, :], b1.rearrange("e (c p) -> (e c) p", p=P)).then_inc(s["small_in"], 16)
            act.dma_start(gate_raw[:, :], gate_w).then_inc(s["small_in"], 16)
            act.dma_start(b2_sb[:, :], b2).then_inc(s["small_in"], 16)
            act.wait_ge(s["small_in"], 80)
            act.activation(tanh_g[:, :], gates[:, :], ACT.Tanh).then_inc(s["gates_t"], 1)
            act.wait_ge(s["ps_wT"], 1)
            act.activation(WqT[:, :, :].rearrange("p k c -> p (k c)"), ps_sel[:, 0, :], ACT.Copy).then_inc(s["wT"], 1)
            act.activation(WkvT[:, 0, :], ps_sel[:, 1, :], ACT.Copy).then_inc(s["wT"], 1)
            act.activation(WkvT[:, 1, :], ps_sel[:, 2, :], ACT.Copy).then_inc(s["wT"], 1)
            act.activation(WoT[:, :, :].rearrange("p k c -> p (k c)"), ps_sel[:, 3, :], ACT.Copy).then_inc(s["wT"], 1)
            act.wait_ge(s["ps_small"], 1)
            act.activation(gateT[:, :, :].rearrange("p k c -> p (k c)"), ps_a[:, 0:KC * E], ACT.Copy)\
                .then_inc(s["small_T"], 1)
            act.activation(b1T[:, :], ps_a[:, 64:64 + E * FC], ACT.Copy).then_inc(s["small_T"], 1)
            for b in range(B):
                act.wait_ge(s["ctxT_ps"], b + 1)
                act.activation(ctxT[b % 2][:, :, :].rearrange("p k c -> p (k c)"),
                               ps[:, b % 2, 0:256], ACT.Copy).then_inc(s["ctxT_sb"], 1)
                act.wait_ge(s["kv_ps"], b + 1)
                act.activation(kv3[:, 0, b, :], ps_o, ACT.Copy).then_inc(s["kv_hi"], 1)
                act.wait_ge(s["kv_r"], b + 1)
                act.activation(kv3[:, 1, b, :], kv_rest, ACT.Copy).then_inc(s["kv_mid"], 1)

            general = flag(act)

            def chunk(n):
                act.wait_ge(s["g_ctxT_ps"], n + 1)
                act.activation(ctxT_g.rearrange("p k c -> p (k c)"), ps_t[:, 0:256], ACT.Copy).then_inc(s["g_ctxT"], 1)
                act.wait_ge(s["g_kv_ps"], n + 1)
                act.activation(kv_g, ps_sel[:, 0, :], ACT.Copy).then_inc(s["g_kv"], 1)

            with act.If(general > 0):
                with act.Fori(0, B * (CHUNKS + 1)) as n:
                    chunk(n)

            def step(t, k, live):
                if live(0):
                    act.wait_ge(s[f"w_in{k}"], (t - k) * 4 + 16)
                    wait_apart(act, "w_lo_ok1", t)
                    act.activation(part_of(t * 2 + 1, 0), raw(t * 2 + 1), ACT.Copy, scale=W_SCALE)\
                        .then_inc(s["w_hi_ok1"], 1)
                    wait_apart(act, "w_hi_ok1", t + 1)
                    act.activation(raw(t * 2 + 1), raw(t * 2 + 1), ACT.Copy, scale=W_SCALE)\
                        .then_inc(s["w_scaled"], 1)
                if live(1):
                    act.wait_ge(s["xnT_ps"], t + 2)
                    wait(act, "q_ps", t + 1)
                    act.activation(xnT[:, :, :].rearrange("p k c -> p (k c)"), ps_t[:, 0:256], ACT.Copy)\
                        .then_inc(s["xnT_ok"], 1)
                if live(-1):
                    act.wait_ge(s["aT_ps"], t)
                    wait(act, "o_ps", t - 1)
                    act.activation(aT[:, :, :].rearrange("p k c -> p (k c)"), ps_a[:, 0:256], ACT.Copy)\
                        .then_inc(s["aT_ok"], 1)
                if live(0):
                    act.wait_ge(s["shifted"], t + 1)
                    act.activation(prob[:, k % 2, :, :].rearrange("p j h -> p (j h)"),
                                   score[:, k % 2, :, :].rearrange("p j h -> p (j h)"), ACT.Exp,
                                   scale=float(HD) ** -0.5).then_inc(s["exped"], 1)
                if live(1):
                    with act.If(general < 1):
                        wait(act, "aT_ps", t)
                        for j in range(WIN):
                            act.wait_ge(s["sel_ps"], t * WIN + (WIN + j + 1))
                            act.activation(sel[:, (k + 1) % 2, j, :], ps_sel[:, j, :], ACT.Copy)\
                                .then_inc(s["sel_ok"], 1)
                if live(0):
                    act.wait_ge(s[f"w_in{k}"], (t - k) * 4 + 16)
                    wait_apart(act, "w_lo_ok0", t)
                    act.activation(part_of(t * 2, 0), raw(t * 2), ACT.Copy, scale=W_SCALE).then_inc(s["w_hi_ok0"], 1)
                if live(-2):
                    act.wait_ge(s["x2T_ps"], t - 1)
                    wait(act, "logit_ps", t - 2)
                    act.activation(x2T[:, :, :].rearrange("p k c -> p (k c)"), ps_t[:, 256:512], ACT.Copy)\
                        .then_inc(s["x2T_ok"], 1)
                    act.wait_ge(s["logit_ps"], t - 1)
                    act.activation(tile_of(logit, t - 2), ps_a[:, 256:256 + E], ACT.Copy).then_inc(s["logit_ok"], 1)

            attention_steps(act, step, 1, 2)

            act.wait_ge(s["rt"], RT_SHIFT)
            act.activation(r_ex[:, :, :], r_tmp[:, :, :], ACT.Exp).then_inc(s["rt_exp"], 1)
            for g in range(4):
                act.wait_ge(s["combT_ps"], g + 1)
                act.activation(r_combT[:, 4 * g:4 * g + 4, :].rearrange("e t p -> e (t p)"), ps_sel[0:E, g, :],
                               ACT.Copy).then_inc(s["combT_ok"], 1)

            def moe(q, k, live):
                if live(0):
                    e = act.value_load(tile_e[0:1, at(q)], min_val=0, max_val=E - 1)
                    biases = b1T[:, bass.ds(e * FC, FC)]
                    wait(act, "hlo_ok", q * 2 - 2)
                    for c in range(FC):
                        if c % 4 == 0:
                            act.wait_ge(s["h_ps"], q * 2 + (c // 4 + 1))
                        act.activation(h32[k][:, c * P:c * P + P], ps_h[k][:, c * P:c * P + P], ACT.Silu,
                                       bias=biases[:, c:c + 1], scale=1.0 / (X_SCALE * W_SCALE))\
                            .then_inc(s["silu_ok"], 1)

            act.wait_ge(s["rt"], RT_LIST)
            expert_steps(act, moe, 0, 0)

        @block.tensor
        def _(pe):
            pe.wait_ge(s["consts"], 8)
            pe.wait_ge(s["wraw_in"], 48)
            for o in range(2):
                for c in range(KC):
                    pe.transpose(ps_sel[:, 0, c * D + o * P:c * D + o * P + P], wq_raw[:, o, c * P:c * P + P], ident[:, :])
                    pe.transpose(ps_sel[:, 3, c * D + o * P:c * D + o * P + P], wo_raw[:, o, c * P:c * P + P], ident[:, :])
            for o in range(4):
                for c in range(KC):
                    mm = pe.transpose(ps_sel[:, 1 + c, o * P:o * P + P], wkv_raw[:, o, c * P:c * P + P], ident[:, :])
            mm.then_inc(s["ps_wT"], 1)
            pe.wait_ge(s["small_in"], 80)
            for c in range(KC):
                pe.transpose(ps_a[:, c * E:c * E + E], gate_raw[:, c * P:c * P + P], ident[0:E, 0:E])
            pe.transpose(ps_a[:, 64:64 + E * FC], b1_raw[:, :], ident[0:E * FC, 0:E * FC]).then_inc(s["ps_small"], 1)
            pe.wait_ge(s["seg_f"], 1)
            pe.wait_ge(s["wT"], 4)
            pe.transpose(ps_sel[:, 3, 0:T], segr[:, :], ident[0:T, 0:T]).then_inc(s["segt_ps"], 1)
            pe.wait_ge(s["ctx_in"], 16)
            for b in range(B):
                wait(pe, "ctxT_sb", b - 1)
                for c in range(KC):
                    mm = pe.transpose(ps[:, b % 2, P * c:P * c + P],
                                      ctx0[:, b, c * P:c * P + P], ident[:, :])
                mm.then_inc(s["ctxT_ps"], 1)
                pe.wait_ge(s["ctxT_sb"], b + 1)
                wait(pe, "kv_r", b)
                for c in range(KC):
                    mm = pe.matmul(ps_o, ctxT[b % 2][:, c, :], WkvT[:, c, :], start=(c == 0), stop=(c == KC - 1))
                mm.then_inc(s["kv_ps"], 1)

            general = flag(pe)

            def chunk(n):
                pe.wait_ge(s["g_ctx"], n * 16 + 16)
                for c in range(KC):
                    mm = pe.transpose(ps_t[:, P * c:P * c + P], ctx_g[:, c * P:c * P + P], ident[:, :])
                mm.then_inc(s["g_ctxT_ps"], 1)
                pe.wait_ge(s["g_ctxT"], n + 1)
                for c in range(KC):
                    mm = pe.matmul(ps_sel[:, 0, :], ctxT_g[:, c, :], WkvT[:, c, :], start=(c == 0), stop=(c == KC - 1))
                mm.then_inc(s["g_kv_ps"], 1)

            with pe.If(general > 0):
                with pe.Fori(0, B * (CHUNKS + 1)) as n:
                    chunk(n)

            pe.wait_ge(s["kv_done"], B)
            pe.wait_ge(s["setup"], 1)

            def step(t, k, live):
                if live(1):
                    pe.wait_ge(s["xn_ok"], t + 2)
                    wait(pe, "xnT_ok", t + 1)
                    for c in range(KC):
                        mm = pe.transpose(ps_t[:, c * P:c * P + P], xn[:, c * P:c * P + P], ident[:, :])
                    mm.then_inc(s["xnT_ps"], 1)
                if live(-1):
                    pe.wait_ge(s["v_ok"], t)
                    wait(pe, "aT_ok", t - 1)
                    wait(pe, "logit_ok", t - 2)
                    for c in range(KC):
                        for j in range(WIN):
                            mm = pe.matmul(ps_a[:, c * P:c * P + P], sel[:, (k + 1) % 2, j, D + c * P:D + c * P + P],
                                           ident[:, :], start=(j == 0), stop=(j == WIN - 1))
                    mm.then_inc(s["aT_ps"], 1)
                if live(1):
                    with pe.If(general < 1):
                        pe.wait_ge(s["hot_ok"], t + 2)
                        for j in range(WIN):
                            wait(pe, "sel_ok", t * WIN + (j + 1))
                            for m in range(3):
                                if isinstance(t, int):
                                    rows = kv3[:, m, (t + 1) // TPB, :]
                                else:
                                    rows = kv3[:, m, bass.ds(pe_batch[0] + (1 if k == 3 else 0), 1), :]\
                                        .rearrange("p o c -> p (o c)")
                                mm = pe.matmul(ps_sel[:, j, :], onehot[:, (k + 1) % 2, j, :], rows,
                                               start=(m == 0), stop=(m == 2))
                            mm.then_inc(s["sel_ps"], 1)
                    pe.wait_ge(s["xnT_ok"], t + 2)
                    wait(pe, "kprod", t + 1)
                    for c in range(KC):
                        mm = pe.matmul(ps_q[:, 0:D], xnT[:, c, :], WqT[:, c, :], start=(c == 0), stop=(c == KC - 1))
                    mm.then_inc(s["q_ps"], 1)
                if live(-1):
                    pe.wait_ge(s["aT_ok"], t)
                    wait(pe, "x1_ok", t - 1)
                    for c in range(KC):
                        mm = pe.matmul(ps_o[:, 0:D], aT[:, c, :], WoT[:, c, :], start=(c == 0), stop=(c == KC - 1))
                    mm.then_inc(s["o_ps"], 1)
                if live(-2):
                    pe.wait_ge(s["x2_ok"], t - 1)
                    for c in range(KC):
                        mm = pe.transpose(ps_t[:, 256 + c * P:256 + c * P + P], x2[:, c * P:c * P + P], ident[:, :])
                    mm.then_inc(s["x2T_ps"], 1)
                    pe.wait_ge(s["x2T_ok"], t - 1)
                    for c in range(KC):
                        mm = pe.matmul(ps_a[:, 256:256 + E], x2T[:, c, :], gateT[:, c, :],
                                       start=(c == 0), stop=(c == KC - 1))
                    mm.then_inc(s["logit_ps"], 1)

            pe_batch = [None]

            def attention_pe():
                def fixed(t):
                    step(t, t % 4, lambda d: 0 <= t + d < T)
                for t in range(-1, 4):
                    fixed(t)
                with pe.Fori(1, 3) as b:
                    pe_batch[0] = b
                    for k in range(4):
                        step(b * 4 + k, k, lambda d: True)
                for t in range(12, T + 2):
                    fixed(t)

            attention_pe()

            pe.wait_ge(s["rt"], RT_PAIRS)
            m16 = r_m16[:, :, :].rearrange("p t e -> p (t e)")
            pe.matmul(ps_q[:, 0:P], before[:, :], m16, start=True, stop=True)
            pe.matmul(ps_q[:, P:2 * P], ones16[:, :], m16, start=True, stop=True).then_inc(s["rt_ps"], 1)
            pe.wait_ge(s["rt"], RT_COMB)
            for t in range(T):
                mm = pe.transpose(ps_sel[0:E, t // 4, (t % 4) * P:(t % 4) * P + P], r_comb[:, t, :], ident[:, :])
                if t % 4 == 3:
                    mm.then_inc(s["combT_ps"], 1)
            pe.wait_ge(s["rt"], RT_HOT)
            for n in range(2 * T):
                mm = pe.matmul(ps_o[:, 0:2 * NT], row_hot[:, n, :],
                               col_val[:, n, :, :].rearrange("p a q -> p (a q)"),
                               start=(n == 0), stop=(n == 2 * T - 1))
            mm.then_inc(s["list_ps"], 1)
            pe.wait_ge(s["combT_ok"], 4)
            for t in range(T):
                bank = ps_a if t % 2 == 0 else ps_t
                wait(pe, "acc_ok", t - 1)
                pe.matmul(bank[:, 0:D], r_combT[:, t, :], b2_sb[:, :], start=True, stop=True).then_inc(s["b2_ps"], 1)

            pe.wait_ge(s["w_lo_ok0"], T)
            pe.wait_ge(s["w_lo_ok1"], T)
            pe.wait_ge(s["acc_ok"], T)
            expert_of = [pe.alloc_register(f"expert_{n}") for n in range(2)]
            expert_before = [pe.alloc_register(f"expert_before_{n}") for n in range(2)]

            w_bytes = w_parts[:, :, :, :].rearrange("p u a c -> p (u a c)").bitcast(U8)

            def expert_byte(register):
                return pe.snap(pe.snap(register, min_val=0, max_val=E - 1) * (4 * 2 * UC * 2))

            def weights_at(first, unit, part, column, n):
                return w_bytes[:, bass.ds(first + (((unit * 2 + part) * UC + column) * 2), n * 2)].bitcast(F16)

            def moe(q, k, live):
                n = (k + 1) % 2
                if live(1):
                    if isinstance(q, int) and q == -1:
                        pe.reg_load(expert_of[n], tile_e[0:1, q + 1:q + 2])
                    up_first = expert_byte(expert_of[n])
                    pe.wait_ge(s["xT_ok"], q + 2)
                    wait(pe, "silu_ok", q * FC)
                if live(-1):
                    down_first = expert_byte(expert_before[n])
                    wait(pe, "y_ok", q - 2)
                for c in range(FC):
                    if live(1):
                        products = []
                        for kc in range(KC):
                            hi = weights_at(up_first, kc, 0, c * P, P)
                            lo = weights_at(up_first, kc, 1, c * P, P)
                            products += [(hi, xT[n][:, kc, :]), (hi, xT[n][:, KC + kc, :]), (lo, xT[n][:, kc, :])]
                        for i, (w, xx) in enumerate(products):
                            mm = pe.matmul(ps_h[n][:, c * P:c * P + P], w, xx, start=(i == 0),
                                           stop=(i == len(products) - 1))
                        if c % 4 == 3:
                            mm.then_inc(s["h_ps"], 1)
                    if live(-1):
                        if c % 4 == 0:
                            pe.wait_ge(s["hlo_ok"], q * 2 + (c // 4 - 1))
                        rhi = weights_at(down_first, KC + c // 4, 0, c % 4 * D, D)
                        rlo = weights_at(down_first, KC + c // 4, 1, c % 4 * D, D)
                        hi, lo = h_hi[n][:, c * P:c * P + P], h_lo[n][:, c * P:c * P + P]
                        pe.matmul(ps_y[n][:, 0:D], hi, rhi, start=(c == 0), stop=False)
                        pe.matmul(ps_y[n][:, 0:D], hi, rlo, start=False, stop=False)
                        mm = pe.matmul(ps_y[n][:, 0:D], lo, rhi, start=False, stop=(c == FC - 1))
                        if c == FC - 1:
                            mm.then_inc(s["y_ps"], 1)
                    if live(2) and c == FC // 2:
                        wait(pe, f"gathered{k}", half_count(q + 2, k))
                        wait(pe, "xT_ok", q + 2)
                        for h in range(4):
                            mm = pe.transpose(ps_x16[:, h * P:h * P + P], xg[k][:, h * P:h * P + P], ident16[:, :])
                        mm.then_inc(s["xT_ps"], 1)
                if k == 1:
                    for m in range(2):
                        if live(m):
                            pe.reg_mov(expert_before[(k + m) % 2], expert_of[(k + m) % 2])
                    if live(3):
                        both = slice(q + 2, q + 4) if isinstance(q, int) else bass.ds(q + 2, 2)
                        pe.reg_load([expert_of[1], expert_of[0]], tile_e[0:1, both])

            expert_steps(pe, moe, 2, 1)

        @block.vector
        def _(dve):
            v = nc.vector
            dve.wait_ge(s["consts"], 13)
            v.tensor_copy(ident16[:, :], ident[:, :]).then_inc(s["cast_consts"], 1)
            v.tensor_copy(iota[:, :], iota_i[:, :]).then_inc(s["cast_consts"], 1)
            v.tensor_copy(part[:, :], part_i[:, :]).then_inc(s["cast_consts"], 1)
            v.tensor_copy(tok1[:, :], tok_i[:, :]).then_inc(s["cast_consts"], 1)
            dve.wait_ge(s["cast_consts"], 4)
            v.tensor_scalar(pad_row[:, :], part[:, 0:1], float(N_TOK + 1), None, ALU.add).then_inc(s["cast_consts"], 1)
            dve.wait_ge(s["seg_in"], 32)
            v.tensor_copy(segr[:, :], segr_i[:, :]).then_inc(s["seg_f"], 1)
            v.tensor_scalar(seg16[:, :], seg_i, 2047.0, -8.0, ALU.min, ALU.max).then_inc(s["seg_cast"], 1)
            dve.wait_ge(s["seg_cast"], 1)
            v.tensor_reduce(seg_max[:, :], seg16[:, :], AX_X, ALU.max).then_inc(s["seg_cast"], 1)
            dve.wait_ge(s["seg_cast"], 2)
            v.tensor_scalar(general_i[:, :], seg_max[:, :], float(P), None, ALU.is_ge).then_inc(s["seg_flag"], 1)
            dve.wait_ge(s["segt_ps"], 1)
            v.tensor_copy(segt[:, :], ps_sel[:, 3, 0:T]).then_inc(s["seg_cast"], 1)
            dve.wait_ge(s["seg_cast"], 3)
            for j in range(WIN):
                v.tensor_scalar(mask[:, :, j], segt[:, :], float(j), MASKED, ALU.is_lt, ALU.mult)
                v.tensor_scalar(win_f[:, :, j], segt[:, :], float(-j), 0.0, ALU.add, ALU.max).then_inc(s["seg_cast"], 1)
            dve.wait_ge(s["seg_cast"], 3 + WIN)
            for b in range(B):
                last = v.tensor_scalar(win_i[:, TPB * b:TPB * b + TPB, :], win_f[:, TPB * b:TPB * b + TPB, :],
                                       float(CTX - 1), float(b * CTX), ALU.min, ALU.add)
            last.then_inc(s["setup"], 1)

            for b in range(B):
                dve.wait_ge(s["kv_hi"], b + 1)
                v.tensor_tensor(kv_rest, ps_o, kv3[:, 0, b, :], ALU.subtract).then_inc(s["kv_r"], 1)
                dve.wait_ge(s["kv_mid"], b + 1)
                v.tensor_tensor(kv3[:, 2, b, :], kv_rest, kv3[:, 1, b, :], ALU.subtract).then_inc(s["kv_done"], 1)
                if b < B - 1:
                    dve.wait_ge(s["kv_done"], b + 1)

            for b in range(B):
                dve.wait_ge(s[f"x_in{b}"], 16)
                for t in range(TPB * b, TPB * b + TPB):
                    v.bn_stats(st1[:, t, :], xs[:, t, :]).then_inc(s["stats1"], 1)
            for t in range(T):
                dve.wait_ge(s["stats1"], t + 1)
                v.bn_aggr(mv1[:, t, :], st1[:, t, :]).then_inc(s["aggr1"], 1)
            dve.wait_ge(s["rstd1_ok"], 1)
            dve.wait_ge(s["gates_t"], 1)

            general = flag(dve)

            def step(t, k, live):
                c, n = k % 2, (k + 1) % 2
                if live(0):
                    keys = sel[:, c, :, 0:D]
                    dve.wait_ge(s["q_ps"], t + 1)
                    dve.wait_ge(s["sel_ok"], t * WIN + WIN)
                    v.tensor_tensor(keys, keys, spread_mid(ps_q[:, 0:D], WIN), ALU.mult).then_inc(s["kprod"], 1)
                if live(-2):
                    dve.wait_ge(s["rstd2_ok"], t - 1)
                    wait(dve, "x2T_ps", t - 2)
                    row = tile_of(xs, t - 2)
                    v.tensor_scalar(x2[:, :], row, mv2[:, c, 0:1], rstd2[:, c, :], ALU.subtract, ALU.mult)\
                        .then_inc(s["x2_ok"], 1)
                if live(0):
                    dve.wait_ge(s["kprod"], t + 1)
                    v.tensor_reduce(score[:, c, :, :], keys.rearrange("p j (h d) -> p j h d", d=HD), AX_X, ALU.add)\
                        .then_inc(s["scored"], 1)
                if live(-2):
                    dve.wait_ge(s["x2_ok"], t - 1)
                    wait(dve, f"xd_out{c}", half_count(t - 4, c))
                    v.tensor_scalar(xsplit[:, c, 0:D], x2[:, :], X_SCALE, None, ALU.mult).then_inc(s["x2hi_ok"], 1)
                if live(0):
                    dve.wait_ge(s["scored"], t + 1)
                    m = tile_of(mask, t).rearrange("p (j o) -> p j o", o=1).to_broadcast([P, WIN, HEADS])
                    v.tensor_tensor(score[:, c, :, :], score[:, c, :, :], m, ALU.add).then_inc(s["masked"], 1)
                if live(-2):
                    dve.wait_ge(s["x2hi_ok"], t - 1)
                    v.scalar_tensor_tensor(out=xsplit[:, c, D:2 * D], in0=x2[:, :], scalar=X_SCALE,
                                           in1=xsplit[:, c, 0:D], op0=ALU.mult, op1=ALU.subtract)\
                        .then_inc(s["xsplit_ok"], 1)
                if live(0):
                    dve.wait_ge(s["masked"], t + 1)
                    v.tensor_reduce(top[:, :], score[:, c, :, :].rearrange("p j h -> p h j"), AX_X, ALU.max)\
                        .then_inc(s["topped"], 1)
                    dve.wait_ge(s["topped"], t + 1)
                    v.tensor_tensor(score[:, c, :, :], score[:, c, :, :], spread_mid(top[:, :], WIN), ALU.subtract)\
                        .then_inc(s["shifted"], 1)
                if live(2):
                    with dve.If(general < 1):
                        wait(dve, "sel_ps", t * WIN + WIN)
                        for j in range(WIN):
                            if isinstance(t, int):
                                sg = seg16[:, (t + 2) * P:(t + 3) * P]
                            else:
                                sg = seg16[:, bass.ds((t + 2) * P, P)]
                            last = v.tensor_scalar(onehot[:, c, j, :], sg, float(j), part[:, j:j + 1],
                                                   ALU.max, ALU.is_equal)
                        last.then_inc(s["hot_ok"], 1)
                if live(0):
                    dve.wait_ge(s["exped"], t + 1)
                    v.tensor_reduce(den[:, :], prob[:, c, :, :].rearrange("p j h -> p h j"), AX_X, ALU.add)\
                        .then_inc(s["summed"], 1)
                if live(2):
                    wait(dve, "xnT_ps", t + 2)
                    v.tensor_scalar(xn[:, :], tile_of(xs, t + 2), mv1[:, at(t + 2), 0], rstd1[:, at(t + 2)],
                                    ALU.subtract, ALU.mult).then_inc(s["xn_ok"], 1)
                if live(0):
                    dve.wait_ge(s["summed"], t + 1)
                    v.reciprocal(rden[:, :], den[:, :]).then_inc(s["inverted"], 1)
                    dve.wait_ge(s["inverted"], t + 1)
                    v.tensor_tensor(prob[:, c, :, :], prob[:, c, :, :], spread_mid(rden[:, :], WIN), ALU.mult)\
                        .then_inc(s["prob_ok"], 1)
                if live(-1):
                    dve.wait_ge(s["o_ps"], t)
                    row = tile_of(xs, t - 1)
                    v.scalar_tensor_tensor(out=row, in0=ps_o[:, 0:D], scalar=tanh_g[:, 0:1], in1=row,
                                           op0=ALU.mult, op1=ALU.add).then_inc(s["x1_ok"], 1)
                    wait_apart(dve, "x1_ok", t)
                    v.bn_stats(st2[:, :], row).then_inc(s["stats2"], 1)
                    wait_apart(dve, "stats2", t)
                    v.bn_aggr(mv2[:, n, :], st2[:, :]).then_inc(s["aggr2"], 1)
                if live(0):
                    dve.wait_ge(s["w_hi_ok0"], t + 1)
                    v.scalar_tensor_tensor(out=part_of(t * 2, 1), in0=raw(t * 2), scalar=W_SCALE,
                                           in1=part_of(t * 2, 0), op0=ALU.mult, op1=ALU.subtract)\
                        .then_inc(s["w_lo_ok0"], 1)

            attention_steps(dve, step, 2, 2)

            done = [0]

            def link(ins):
                done[0] += 1
                ins.then_inc(s["rt"], 1)
                dve.wait_ge(s["rt"], done[0])

            def by_expert(ap):
                return ap.rearrange("p (t o) -> p t o", o=1).to_broadcast([P, T, E])

            dve.wait_ge(s["logit_ok"], T)
            link(v.tensor_reduce(r_mx[:, :], logit[:, :, :], AX_X, ALU.max))
            link(v.tensor_tensor(r_tmp[:, :, :], logit[:, :, :], by_expert(r_mx[:, :]), ALU.subtract))
            assert done[0] == RT_SHIFT
            dve.wait_ge(s["rt_exp"], 1)
            link(v.tensor_reduce(r_sum[:, :], r_ex[:, :, :], AX_X, ALU.add))
            link(v.reciprocal(r_rs[:, :], r_sum[:, :]))
            link(v.tensor_tensor(r_p[:, :, :], r_ex[:, :, :], by_expert(r_rs[:, :]), ALU.mult))
            for t in range(T):
                ins = v.max(r_m8[:, t, :], r_p[:, t, :])
            link(ins)
            for t in range(T):
                ins = v.max_index(r_i8[:, t, :], r_m8[:, t, :], r_p[:, t, :])
            link(ins)
            link(v.tensor_copy(r_i2[:, :, :], r_i8[:, :, 0:2]))
            experts = spread_mid(iota[:, 0:E], T)
            for a in range(2):
                ins = v.tensor_tensor(r_oh[:, a, :, :], r_i2[:, :, a:a + 1].to_broadcast([P, T, E]), experts,
                                      ALU.is_equal)
            link(ins)
            link(v.tensor_tensor(r_m16[:, :, :], r_oh[:, 0, :, :], r_oh[:, 1, :, :], ALU.add))
            assert done[0] == RT_PAIRS
            for a in range(2):
                ins = v.tensor_scalar(r_w[:, a, :], r_m8[:, :, a], tanh_g[:, 1:2], None, ALU.mult)
            link(ins)
            for a in range(2):
                ins = v.tensor_tensor((r_ex, r_tmp)[a][:, :, :], r_oh[:, a, :, :], by_expert(r_w[:, a, :]), ALU.mult)
            link(ins)
            link(v.tensor_tensor(r_comb[:, :, :], r_ex[:, :, :], r_tmp[:, :, :], ALU.add))
            assert done[0] == RT_COMB
            dve.wait_ge(s["rt_ps"], 1)
            totals = ps_q[:, P:2 * P].rearrange("p (t e) -> p e t", e=E)
            link(v.tensor_copy(r_tot[:, :, :], totals))
            link(v.tensor_tensor_scan(r_inc[:, :, :].rearrange("p e t -> p (e t)"),
                                      r_go[:, :, :].rearrange("p e t -> p (e t)"),
                                      r_tot[:, :, :].rearrange("p e t -> p (e t)"), 0.0, ALU.mult, ALU.add))
            link(v.tensor_tensor(r_exc[:, :, :], r_inc[:, :, :], r_tot[:, :, :], ALU.subtract))
            link(v.tensor_scalar(r_ni[:, :], r_inc[:, :, T - 1], float(P - 1), None, ALU.add))
            link(v.tensor_scalar(r_ti[:, :], r_ni[:, :], 7, None, ALU.logical_shift_right))
            link(v.tensor_copy(r_tf[:, :], r_ti[:, :]))
            link(v.tensor_tensor_scan(r_end[:, :], r_one[:, :], r_tf[:, :], 0.0, ALU.mult, ALU.add))
            link(v.tensor_tensor(r_start[:, :], r_end[:, :], r_tf[:, :], ALU.subtract))
            link(v.tensor_scalar(r_start[:, :], r_start[:, :], float(P), None, ALU.mult))
            link(v.tensor_tensor(r_base[:, :, :], ps_q[:, 0:P].rearrange("p (t e) -> p t e", e=E),
                                 r_exc[:, :, :].rearrange("p e t -> p t e"), ALU.add))
            link(v.tensor_tensor(r_base[:, :, :], r_base[:, :, :], spread_mid(r_start[:, :], T), ALU.add))
            for a in range(2):
                link(v.tensor_tensor(r_tmp[:, :, :], r_oh[:, a, :, :], r_base[:, :, :], ALU.mult))
                link(v.tensor_reduce(r_slot[:, a, :], r_tmp[:, :, :], AX_X, ALU.add))
            link(v.tensor_copy(r_si[:, :, :], r_slot[:, :, :]))
            v.tensor_scalar(r_qi[:, :, :], r_si[:, :, :], 7, None, ALU.logical_shift_right)
            link(v.tensor_scalar(r_ri[:, :, :], r_si[:, :, :], P - 1, None, ALU.bitwise_and))
            v.tensor_copy(r_q[:, :, :], r_qi[:, :, :])
            link(v.tensor_copy(r_r[:, :, :], r_ri[:, :, :]))
            link(v.tensor_scalar(r_w[:, :, :], r_w[:, :, :], 1.0 / (H_SCALE * W_SCALE), None, ALU.mult))
            dve.wait_ge(s["aT_ps"], T)
            r_all = r_r[:, :, :].rearrange("p a t -> p (a t)").rearrange("p (n o) -> p n o", o=1)
            q_all = r_q[:, :, :].rearrange("p a t -> p (a t)").rearrange("p (n o) -> p n o", o=1)
            w_all = r_w[:, :, :].rearrange("p a t -> p (a t)").rearrange("p (n o) -> p n o", o=1)
            v.tensor_tensor(row_hot, spread_mid(iota[:, :], 2 * T), r_all.to_broadcast([P, 2 * T, P]), ALU.is_equal)
            link(v.tensor_tensor(col_val[:, :, 0, :], spread_mid(iota[:, 0:NT], 2 * T),
                                 q_all.to_broadcast([P, 2 * T, NT]), ALU.is_equal))
            link(v.tensor_tensor(col_val[:, :, 1, :], col_val[:, :, 0, :], w_all.to_broadcast([P, 2 * T, NT]), ALU.mult))
            for a in range(2):
                half_val = col_val[:, T * a:T * a + T, 0, :]
                ins = v.tensor_tensor(half_val, half_val,
                                      tok1[:, :].rearrange("p (t o) -> p t o", o=1).to_broadcast([P, T, NT]), ALU.mult)
            link(ins)
            assert done[0] == RT_HOT
            tiles = iota[:, 0:NT].rearrange("p (q o) -> p q o", o=1).to_broadcast([P, NT, E])
            for n in range(2):
                dve.wait_ge(s[f"xd_out{n}"], 16 * T // 2)
            link(v.tensor_tensor(l_cmp[:, :, :], spread_mid(r_end[:, :], NT), tiles, ALU.is_le))
            link(v.tensor_reduce(l_e[:, :], l_cmp[:, :, :], AX_X, ALU.add))
            link(v.tensor_scalar(tile_e[:, :], l_e[:, :], float(E - 1), None, ALU.min))
            dve.wait_ge(s["list_ps"], 1)
            link(v.tensor_scalar(l_empty[:, :], ps_o[:, 0:NT], 0.5, pad_row[:, 0:1], ALU.is_lt, ALU.mult))
            link(v.tensor_scalar(l_idx[:, :], ps_o[:, 0:NT], -1.0, None, ALU.add))
            v.tensor_copy(slot_w[:, :], ps_o[:, NT:2 * NT])
            link(v.tensor_tensor(slot_row[:, :], l_idx[:, :], l_empty[:, :], ALU.add))
            assert done[0] == RT_LIST
            for t in range(T):
                dve.wait_ge(s["b2_ps"], t + 1)
                bank = ps_a if t % 2 == 0 else ps_t
                v.tensor_tensor(xs[:, t, :], bank[:, 0:D], xs[:, t, :], ALU.add).then_inc(s["acc_ok"], 1)

            def moe(q, k, live):
                if live(0):
                    for h in range(2):
                        cols = slice(512 * h, 512 * h + 512)
                        dve.wait_ge(s["silu_ok"], q * FC + 4 * (h + 1))
                        wait(dve, "y_ps", q - 1)
                        v.tensor_scalar(h_hi[k][:, cols], h32[k][:, cols], H_SCALE, None, ALU.mult)\
                            .then_inc(s["hhi_ok"], 1)
                        dve.wait_ge(s["hhi_ok"], q * 2 + (h + 1))
                        v.scalar_tensor_tensor(out=h_lo[k][:, cols], in0=h32[k][:, cols], scalar=H_SCALE,
                                               in1=h_hi[k][:, cols], op0=ALU.mult, op1=ALU.subtract)\
                            .then_inc(s["hlo_ok"], 1)
                if live(2):
                    dve.wait_ge(s["xT_ps"], q + 3)
                    wait(dve, "h_ps", q * 2 + 2)
                    v.tensor_copy(xT[k].rearrange("p a c -> p (a c)"), ps_x16[:, 0:512]).then_inc(s["xT_ok"], 1)
                if live(-1):
                    n = (k + 1) % 2
                    dve.wait_ge(s["y_ps"], q)
                    wait(dve, "scattered", q * 16 - 32)
                    v.tensor_scalar(y_sb[n], ps_y[n][:, 0:D], slot_w[:, at(q - 1)], None, ALU.mult)\
                        .then_inc(s["y_ok"], 1)

            expert_steps(dve, moe, 2, 1)


RT_SHIFT, RT_PAIRS, RT_COMB, RT_HOT, RT_LIST = 2, 10, 13, 35, 41

_INS = ["x", "ctx_1024", "itok_BxS_0_511", "g_xattn", "g_ffn", "L0_xattn_Wq", "L0_xattn_Wkv", "L0_xattn_Wo",
        "L0_ffn_gate_w", "L0_ffn_w1", "L0_ffn_b1", "L0_ffn_w2", "L0_ffn_b2"]


def kernel(**inputs):
    import numpy as _np
    import concourse.bacc as _bacc
    from concourse import mybir as _mybir
    from concourse.bass_utils import run_bass_kernel_spmd as _run

    nc = _bacc.Bacc("TRN2", target_bir_lowering=False, num_devices=1)
    arrays, args = {}, []
    for name in _INS:
        a = _np.ascontiguousarray(inputs[name])
        arrays[f"in_{name}"] = a
        args.append(nc.dram_tensor(f"in_{name}", a.shape, _mybir.dt.from_np(a.dtype), kind="ExternalInput").ap())
    shape = inputs["x"].shape
    args.append(nc.dram_tensor("out_0", shape, _mybir.dt.float32, kind="ExternalOutput").ap())
    flamingo_layer(nc, *args)
    r = _run(nc, [arrays], core_ids=[0])
    return r.results[0]["out_0"]
```

```python
from contextlib import ExitStack, nullcontext

import concourse.bass as bass
from concourse import mybir

P = 128
F32 = mybir.dt.float32
F16 = mybir.dt.float16
BF16 = mybir.dt.bfloat16
I32 = mybir.dt.int32
U8 = mybir.dt.uint8
U32 = mybir.dt.uint32
ALU = mybir.AluOpType
ACT = mybir.ActivationFunctionType
AX_X = mybir.AxisListType.X

HEADS, WIN, TOP_K = 16, 4, 2
EPS = 1e-5
MASKED = -3.0e38
X_SCALE, W_SCALE, H_SCALE = 64.0, 64.0, 4.0
W_UNSCALE = 1.0 / (H_SCALE * W_SCALE) / W_SCALE


def flamingo_layer(nc, x, ctx_in, seg, g_xattn, g_ffn, Wq, Wkv, Wo, gate_w, w1, b1, w2, b2, out):
    B, S, D = x.shape
    CTX = ctx_in.shape[1]
    E, _, F = w1.shape
    T = B * S // P
    TPB = S // P
    HD = D // HEADS
    KC = D // P
    FC = F // P
    NT = T * TOP_K + E - 1
    FULL = T * TOP_K
    LAST_LOOPED = (FULL - 3) // 4 * 4
    N_TOK = B * S
    CHUNKS = CTX // P
    UNITS = 4 * E
    UC = KC * F // 2
    assert TPB == 4 and KC == 2 and FC == 8 and T == 16 and UNITS == 2 * T and D == 256

    xd = nc.dram_tensor("tokens_split", (N_TOK + P, 2 * D), F16).ap()
    acc = nc.dram_tensor("rows_sum", (N_TOK + P, D), F32).ap()
    kvd = nc.dram_tensor("keys_values", (B * CTX, 2 * D), F32).ap()

    x_v = x.rearrange("b (t p) d -> p (b t) d", p=P)
    seg_row = seg.rearrange("b s -> (b s)").rearrange("(o n) -> o n", o=1)
    seg_tiles = seg.rearrange("b (t p) -> (b t) p", p=P)
    ctx_rows = ctx_in.rearrange("b s d -> (b s) d")
    ctx_first = ctx_in[:, 0:P, :].rearrange("b p d -> p b d")
    w1_v = w1.rearrange("e (k p) f -> e p k f", p=P)
    w2_v = w2.rearrange("e (c p) n -> e p c n", p=P)
    xd_v = xd.rearrange("(t p) d -> t p d", p=P)
    acc_v = acc[0:N_TOK, :].rearrange("(t p) d -> p t d", p=P)
    out_rows = out.rearrange("b s d -> (b s) d")

    with ExitStack() as ctx:
        def sb(name, shape, dt):
            return ctx.enter_context(nc.sbuf_tensor(name, shape, dt))

        def sem(name):
            return ctx.enter_context(nc.semaphore(name))

        w_parts = sb("w_parts", [P, UNITS + 2, 2, UC], F16)
        xs = sb("xs", [P, T, D], F32)
        sel = sb("sel", [P, 2, WIN, 2 * D], F32)
        seg16 = sb("seg16", [P, N_TOK], F16)
        onehot = sb("onehot", [P, 2, WIN, P], BF16)
        kv3 = sb("kv3", [P, 3, B, 2 * D], BF16)
        WqT = sb("WqT", [P, KC, D], F32)
        WoT = sb("WoT", [P, KC, D], F32)
        gateT = sb("gateT", [P, KC, E], F32)
        b1T = sb("b1T", [P, E * FC], F32)
        b1_raw = sb("b1_raw", [E * FC, P], F32)
        gate_raw = sb("gate_raw", [E, D], F32)
        b2_sb = sb("b2_sb", [E, D], F32)
        gates = sb("gates", [P, 2], F32)
        tanh_g = sb("tanh_g", [P, 2], F32)
        xn = sb("xn", [P, D], F32)
        xnT = sb("xnT", [P, KC, P], F32)
        aT = sb("aT", [P, KC, P], F32)
        x2 = sb("x2", [P, D], F32)
        x2T = sb("x2T", [P, KC, P], F32)
        xsplit = sb("xsplit", [P, 2, 2 * D], F16)
        ident = sb("ident", [P, P], F32)
        ident16 = sb("ident16", [P, P], F16)
        before = sb("before", [P, P], F16)
        ones16 = sb("ones16", [P, P], F16)
        zeros = onehot[:, 0, :, :].rearrange("p j r -> p (j r)").bitcast(F16)
        iota_i = x2[:, 0:P].bitcast(I32)
        iota = sb("iota", [P, P], F32)
        iota16 = sb("iota16", [P, P], F16)
        tok16 = sb("tok16", [P, T], F16)
        part_i = sb("part_i", [P, WIN], I32)
        part = sb("part", [P, WIN], F32)
        tok_i = sb("tok_i", [P, T], I32)
        half = sb("half", [P, T], F32)
        segr_i = x2[0:T, P:2 * P].bitcast(I32)
        segr = xn[0:T, 0:P]
        segt = sb("segt", [P, T], F32)
        mask = sb("mask", [P, T, WIN], F32)
        win_f = sb("win_f", [P, T, WIN], F32)
        win_i = sb("win_i", [P, T, WIN], I32)
        win_col = sb("win_col", [P, WIN, 1], I32)
        seg_max = sb("seg_max", [1, 1], F32)
        general_i = sb("general_i", [1, 1], I32)
        st1 = sb("st1", [P, T, 6], F32)
        mv1 = sb("mv1", [P, T, 2], F32)
        rstd1 = sb("rstd1", [P, T], F32)
        st2 = sb("st2", [P, 6], F32)
        mv2 = sb("mv2", [P, 2, 2], F32)
        var2 = sb("var2", [P, 1], F32)
        rstd2 = sb("rstd2", [P, 2, 1], F32)
        score = sb("score", [P, 2, WIN, HEADS], F32)
        prob = sb("prob", [P, 2, WIN, HEADS], F32)
        top = sb("top", [P, HEADS], F32)
        den = sb("den", [P, HEADS], F32)
        rden = sb("rden", [P, HEADS], F32)
        logit = sb("logit", [P, T, E], F32)

        sel0 = sel[:, 0, :, :].rearrange("p j c -> p (j c)")
        sel1 = sel[:, 1, :, :].rearrange("p j c -> p (j c)")
        wq_raw = sel0[:, 0:512].rearrange("p (o c) -> p o c", o=2)
        wkv_raw = sel0[:, 512:1536].rearrange("p (o c) -> p o c", o=4)
        wo_raw = sel0[:, 1536:2048].rearrange("p (o c) -> p o c", o=2)
        ctx0 = sel1[:, 0:1024].rearrange("p (b d) -> p b d", b=B)
        WkvT = sel1[:, 1024:2048].rearrange("p (k c) -> p k c", k=KC)
        ctx_g = sel1[:, 0:256]
        ctxT_g = sel1[:, 256:512].rearrange("p (k c) -> p k c", k=KC)
        kv_g = sel1[:, 512:1024]
        last_places = w_parts[:, UNITS:UNITS + 2, :, :].rearrange("p u a c -> p (u a c)")
        seg_i = last_places[0:1, :].bitcast(I32)
        kv_rest = [xsplit[:, :, :].rearrange("p a c -> p (a c)").bitcast(F32), sel0[:, 512:1024]]
        ctxT = [x2T, aT, xnT, sel0[:, 0:256].rearrange("p (k c) -> p k c", k=KC)]

        row_hot = sel0.bitcast(F16).rearrange("p (n r) -> p n r", r=P)
        kv_words = kv3[:, :, :, :].rearrange("p a b c -> p (a b c)").bitcast(F32)
        col_val = kv3[:, :, :, :].rearrange("p a b c -> p (a b c)").bitcast(F16)[:, 0:2 * T * 3 * NT]\
            .rearrange("p (n i q) -> p n i q", i=3, q=NT)
        b2_rows = [w[:, i, :] for w in (WqT, WoT) for i in range(2)]
        flat_x2T = x2T[:, :, :].rearrange("p k c -> p (k c)")
        flat_aT = aT[:, :, :].rearrange("p k c -> p (k c)")
        spare = seg16[:, :].bitcast(F32)

        def over(i, *dims, spare=spare):
            names = " ".join("abc"[:len(dims)])
            n = 1
            for d in dims:
                n *= d
            return spare[:, i:i + n].rearrange(f"p ({names}) -> p {names}", **dict(zip("abc", dims)))

        r_mx = sb("r_mx", [P, T], F32)
        r_ex = over(0, T, E, spare=x2[:, :])
        r_sum = sb("r_sum", [P, T], F32)
        r_rs = sb("r_rs", [P, T], F32)
        r_p = over(128, T, E, spare=x2[:, :])
        r_m8 = over(0, T, 8)
        r_i8 = over(128, T, 8).bitcast(U32)
        r_i2 = sb("r_i2", [P, T, 2], F32)
        r_oh = over(256, 2, T, E)
        r_m16 = over(192, T, E // 2, spare=flat_x2T).rearrange("p t e -> p (t e)").bitcast(F16).rearrange("p (t e) -> p t e", t=T)
        r_tot = over(512, E, T)
        r_go = sb("r_go", [P, E, T], F32)
        r_inc = over(640, E, T)
        r_exc = over(768, E, T)
        r_ni = sb("r_ni", [P, E], I32)
        r_ti = sb("r_ti", [P, E], I32)
        r_tf = sb("r_tf", [P, E], F32)
        r_one = sb("r_one", [P, E], F32)
        r_end = sb("r_end", [P, E], F32)
        r_start = sb("r_start", [P, E], F32)
        r_base = over(896, T, E)
        r_tmp = over(0, T, E, spare=xn[:, :])
        r_slot = over(0, 2, T, spare=flat_aT)
        r_si = over(32, 2, T, spare=flat_aT).bitcast(I32)
        r_qi = over(64, 2, T, spare=flat_aT).bitcast(I32)
        r_ri = over(96, 2, T, spare=flat_aT).bitcast(I32)
        r_pair = flat_aT[:, 128:192].bitcast(F16).rearrange("p (v n) -> p v n", v=4)
        r_w = sb("r_w", [P, 2, T], F32)
        r_comb = over(128, T, E, spare=xn[:, :])
        r_combT = last_places[0:E, :].bitcast(F32).rearrange("e (t p) -> e t p", p=P)
        pad_row = sb("pad_row", [P, 1], F32)
        l_w = flat_x2T[:, 3 * NT:4 * NT]
        l_empty = flat_x2T[:, 0 * NT:1 * NT]
        l_idx = flat_x2T[:, 1 * NT:2 * NT]
        slot_row = sb("slot_row", [P, NT], I32)
        slot_w = sb("slot_w", [P, NT], F32)
        l_cmp = over(0, NT, E, spare=kv_rest[0])
        l_e = flat_x2T[:, 2 * NT:3 * NT]
        tile_e = sb("tile_e", [P, NT], I32)
        tiles_i = sb("tiles_i", [P, 1], I32)
        gcol = sb("gcol", [P, 2, 1], I32)
        scol = sb("scol", [P, 2, 1], I32)

        sel0_16 = sel0.bitcast(F16)
        xg = [sel0_16[:, 512 * i:512 * i + 512] for i in range(2)]
        xT = [sel0_16[:, 1024 + 512 * i:1536 + 512 * i].rearrange("p (a c) -> p a c", a=4) for i in range(2)]
        y_sb = [sel0[:, 1024 + 256 * i:1280 + 256 * i] for i in range(2)]
        y_low = [WqT[:, i, :] for i in range(2)]
        h32 = [sel1[:, 1024 * i:1024 * i + 1024] for i in range(2)]
        kv16 = kv_words.bitcast(F16)
        h_hi = [kv16[:, 1024 * i:1024 * i + 1024] for i in range(2)]
        h_lo = [kv16[:, 2048 + 1024 * i:3072 + 1024 * i] for i in range(2)]

        ps = ctx.enter_context(nc.psum_tensor("ps", [P, 8, 512], F32))
        ps_t = ps[:, 0, :]
        ps_q = ps[:, 1, :]
        ps_sel = ps[:, 2:6, :]
        ps_a = ps[:, 6, :]
        ps_o = ps[:, 7, :]
        ps_ctxT = [ps_t, ps_q, ps_o, ps_a]
        b2_bank = [ps_a, ps_t, ps_sel[:, 0, :], ps_sel[:, 1, :]]
        ps_x16 = ps[:, 0, :].bitcast(F16)
        ps_h = [ps[:, 1:3, :].rearrange("p a c -> p (a c)"), ps[:, 3:5, :].rearrange("p a c -> p (a c)")]
        ps_y = [ps[:, 5, :], ps[:, 6, :]]

        names = """unused x_in0 x_in1 x_in2 x_in3 seg_in wraw_in small_in ctx_in w_in0 w_in1 w_in2 w_in3 consts cast_consts
            seg_cast seg_f segt_ps seg_ps seg_all setup seg_flag gates_t ps_wT ps_small wT small_T ctxT_ps ctxT_sb
            kv_ps kv_hi kv_r kv_mid kv_done
            g_ctx g_ctxT_ps g_ctxT g_kv_ps g_kv g_stored g_col g_rows
            stats1 aggr1 var1 rstd1_ok xn_ok xnT_ps xnT_ok q_ps hot_ok sel_ps sel_ok
            kprod scored masked topped shifted exped summed inverted prob_ok v_ok aT_ps aT_ok o_ps
            x1_ok stats2 aggr2 var2_ok rstd2_ok x2_ok x2hi_ok xsplit_ok xd_out0 xd_out1 x2T_ps x2T_ok logit_ps logit_ok
            w_scaled w_hi_ok0 w_hi_ok1 w_lo_ok0 w_lo_ok1 zero_out
            rt rt_exp rt_ps list_ps combT_ps combT_ok b2_ps b2_rows_ok acc_ok acc_out
            gcol_ok scol_ok gathered0 gathered1 xT_ps xT_ok h_ps silu_ok hhi_ok hlo_ok y_ps y_low_ok y_ok scattered out_done""".split()
        s = {n: sem(n) for n in names}

        block = ctx.enter_context(nc.Block())

        def wait(eng, name, value):
            if not isinstance(value, int) or value > 0:
                eng.wait_ge(s[name], value)

        def wait_apart(eng, name, value):
            wait(eng, name, value)
            if not isinstance(value, int):
                eng.sem_inc(s["unused"], 1)

        def half_count(t, parity):
            return 8 * (t - parity) + 16

        def attention_steps(eng, step, lead, lag):
            def fixed(t):
                step(t, t % 4, lambda d: 0 <= t + d < T)
            for t in range(-lead, 4):
                fixed(t)
            with eng.Fori(1, 3) as b:
                for k in range(4):
                    step(b * 4 + k, k, lambda d: True)
            for t in range(12, T + lag):
                fixed(t)

        def expert_steps(eng, step, lead, lag):
            def fixed(q):
                step(q, q % 4, lambda d: 0 <= q + d < NT)
            for q in range(-lead, 4):
                fixed(q)
            with eng.Fori(1, LAST_LOOPED // 4) as i:
                for k in range(4):
                    step(i * 4 + k, k, lambda d: True)
            for q in range(LAST_LOOPED, NT + lag):
                fixed(q)

        def tile_count(eng):
            return eng.value_load(tiles_i[0:1, 0:1], min_val=FULL, max_val=NT)

        def filled(eng, tiles, q):
            return eng.If(tiles > q) if isinstance(q, int) and q >= FULL else nullcontext()

        def at(v):
            return slice(v, v + 1) if isinstance(v, int) else bass.ds(v, 1)

        def tile_of(ap, v):
            return ap[:, at(v), :].rearrange("p o c -> p (o c)")

        def spread_mid(ap, n):
            return ap.rearrange("p (o c) -> p o c", o=1).to_broadcast([P, n, ap.shape[1]])

        def raw(u):
            return w_parts[:, at(u + 2), :, :].rearrange("p o a c -> p (o a c)").bitcast(F32)

        def part_of(u, a):
            return w_parts[:, at(u), a, :].rearrange("p o c -> p (o c)")

        def flag(eng):
            eng.wait_ge(s["seg_flag"], 1)
            return eng.value_load(general_i[0:1, 0:1], min_val=0, max_val=1)

        @block.sync
        def _(sp):
            sp.dma_start(segr_i[:, :], seg_tiles).then_inc(s["seg_in"], 16)
            sp.dma_start(seg_i, seg_row).then_inc(s["seg_in"], 16)
            sp.dma_start(wq_raw, Wq.rearrange("(o p) c -> p o c", p=P)).then_inc(s["wraw_in"], 16)
            sp.dma_start(wkv_raw, Wkv.rearrange("(o p) c -> p o c", p=P)).then_inc(s["wraw_in"], 16)
            sp.dma_start(wo_raw, Wo.rearrange("(o p) c -> p o c", p=P)).then_inc(s["wraw_in"], 16)
            sp.dma_start(ctx0, ctx_first).then_inc(s["ctx_in"], 16)
            sp.wait_ge(s["consts"], 6)
            sp.dma_start(xd[N_TOK:N_TOK + P, :], zeros[:, :]).then_inc(s["zero_out"], 16)
            sp.dma_start(acc[N_TOK:N_TOK + P, :], zeros.bitcast(F32)).then_inc(s["zero_out"], 16)

            def chunk(n, row):
                sp.dma_start(ctx_g, ctx_rows[bass.ds(row, P), :]).then_inc(s["g_ctx"], 16)
                sp.wait_ge(s["g_kv"], n + 1)
                sp.dma_start(kvd[bass.ds(row, P), :], kv_g).then_inc(s["g_stored"], 16)
                wait_apart(sp, "g_stored", n * 16 + 16)

            def weights_in(t, k):
                e = t // 2 if isinstance(t, int) else (t - k) // 2 + k // 2
                if k % 2 == 0:
                    src = w1_v[at(e), :, :, :].rearrange("o p k f -> p (o k) f")
                    shape = dict(k=KC)
                else:
                    src = w2_v[at(e), :, :, :].rearrange("o p c n -> p (o c) n")
                    shape = dict(k=FC)
                places = slice(2 * t + 2, 2 * t + 4) if isinstance(t, int) else bass.ds(t * 2 + 2, 2)
                dst = w_parts[:, places, :, :].rearrange("p u a c -> p (u a c)").bitcast(F32)\
                    .rearrange("p (k n) -> p k n", **shape)
                sp.dma_start(dst, src).then_inc(s[f"w_in{k}"], 16)

            for b in range(B):
                sp.wait_ge(s[f"x_in{b}"], 16)
            for t in range(4):
                weights_in(t, t)

            general = flag(sp)
            with sp.If(general > 0):
                sp.wait_ge(s["kv_done"], B)
                with sp.Fori(0, B) as b:
                    with sp.Fori(0, CHUNKS) as c:
                        chunk(b * (CHUNKS + 1) + c, b * CTX + c * P)
                    chunk(b * (CHUNKS + 1) + CHUNKS, b * CTX + (CTX - P))

            sp.wait_ge(s["seg_cast"], 1)

            def step(t, k, live):
                if live(4):
                    wait_apart(sp, f"w_in{k}", (t - k) * 4 + 16)
                    weights_in(t + 4, k)
                if live(-2):
                    wait_apart(sp, "xsplit_ok", t - 1)
                    sp.dma_start(xd_v[at(t - 2), :, :].rearrange("o p d -> p (o d)"),
                                 xsplit[:, k % 2, :]).then_inc(s[f"xd_out{k % 2}"], 16)

            attention_steps(sp, step, 0, 2)

            sp.wait_ge(s["rt"], RT_LIST)
            for b in range(B):
                sp.wait_ge(s["acc_ok"], TPB * (b + 1))
                sp.dma_start(acc_v[:, TPB * b:TPB * b + TPB, :],
                             xs[:, TPB * b:TPB * b + TPB, :]).then_inc(s["acc_out"], 16)
            tiles = tile_count(sp)
            wait_apart(sp, "scattered", tiles * 16)
            sp.dma_start(out_rows, acc[0:N_TOK, :]).then_inc(s["out_done"], 16)
            sp.wait_ge(s["out_done"], 16)
            for n in range(2):
                sp.wait_ge(s[f"xd_out{n}"], 16 * T // 2)
            sp.wait_ge(s["zero_out"], 32)

        @block.gpsimd
        def _(pool):
            pool.memset(ident[:, :], 0.0).then_inc(s["consts"], 1)
            pool.memset(before[:, :], 1.0).then_inc(s["consts"], 1)
            pool.memset(ones16[:, :], 1.0).then_inc(s["consts"], 1)
            pool.memset(half[:, :], -0.5).then_inc(s["consts"], 1)
            pool.memset(r_one[:, :], 1.0).then_inc(s["consts"], 1)
            pool.memset(zeros[:, :], 0.0).then_inc(s["consts"], 1)
            pool.memset(r_go[:, :, :], 1.0).then_inc(s["consts"], 1)
            pool.wait_ge(s["consts"], 7)
            pool.affine_select(out=ident[:, :], in_=ident[:, :], compare_op=ALU.not_equal, fill=1.0, base=0,
                               pattern=[[-1, P]], channel_multiplier=1).then_inc(s["consts"], 1)
            pool.affine_select(out=before[:, :], in_=before[:, :], compare_op=ALU.is_gt, fill=0.0, base=0,
                               pattern=[[1, P]], channel_multiplier=-1).then_inc(s["consts"], 1)
            pool.memset(r_go[:, :, 0:1], 0.0).then_inc(s["consts"], 1)
            pool.iota(iota_i[:, :], pattern=[[1, P]], base=0, channel_multiplier=0).then_inc(s["consts"], 1)
            pool.iota(part_i[:, :], pattern=[[1, WIN]], base=0, channel_multiplier=1).then_inc(s["consts"], 1)
            pool.iota(tok_i[:, :], pattern=[[P, T]], base=1, channel_multiplier=1).then_inc(s["consts"], 1)
            for b in range(B):
                pool.dma_start(xs[:, TPB * b:TPB * b + TPB, :], x_v[:, TPB * b:TPB * b + TPB, :])\
                    .then_inc(s[f"x_in{b}"], 16)
            pool.wait_ge(s["aggr1"], T)
            pool.tensor_scalar(rstd1[:, :], mv1[:, :, 1], EPS, None, ALU.add).then_inc(s["var1"], 1)
            pool.wait_ge(s["var1"], 1)
            pool.tensor_tensor(rstd1[:, :], rstd1[:, :], half[:, :], ALU.pow).then_inc(s["rstd1_ok"], 1)

            general = flag(pool)

            def step(t, k, live):
                if live(1):
                    with pool.If(general > 0):
                        pool.wait_ge(s["g_stored"], 16 * B * (CHUNKS + 1))
                        pool.wait_ge(s["setup"], 1)
                        wait(pool, "aT_ps", t)
                        for j in range(WIN):
                            pool.tensor_copy(win_col[:, j, :], win_i[:, at(t + 1), j]).then_inc(s["g_col"], 1)
                        wait_apart(pool, "g_col", t * WIN + 2 * WIN)
                        for j in range(WIN):
                            pool.indirect_dma_start(sel[:, (k + 1) % 2, j, :], None, kvd,
                                                    bass.IndirectOffsetOnAxis(win_col[:, j, :], 0))\
                                .then_inc(s["g_rows"], 16)
                        pool.wait_ge(s["g_rows"], t * 16 * WIN + 32 * WIN)
                        for j in range(WIN):
                            pool.sem_inc(s["sel_ok"], 1)
                if live(-2):
                    pool.wait_ge(s["x2hi_ok"], t - 1)
                    n = k % 2
                    pool.tensor_tensor(xsplit[:, n, D:2 * D], x2[:, :], xsplit[:, n, 0:D], ALU.subtract)\
                        .then_inc(s["xsplit_ok"], 1)
                if live(0):
                    pool.wait_ge(s["prob_ok"], t + 1)
                    v = sel[:, k % 2, :, D:2 * D].rearrange("p j (h d) -> p j h d", d=HD)
                    pr = prob[:, k % 2, :, :].rearrange("p j (h o) -> p j h o", o=1).to_broadcast([P, WIN, HEADS, HD])
                    pool.tensor_tensor(v, v, pr, ALU.mult).then_inc(s["v_ok"], 1)
                if live(-1):
                    n = (k + 1) % 2
                    wait_apart(pool, "aggr2", t)
                    pool.tensor_scalar(var2[:, :], mv2[:, n, 1:2], EPS, X_SCALE ** -2, ALU.add, ALU.mult).then_inc(s["var2_ok"], 1)
                    pool.wait_ge(s["var2_ok"], t)
                    pool.tensor_tensor(rstd2[:, n, :], var2[:, :], half[:, 0:1], ALU.pow)\
                        .then_inc(s["rstd2_ok"], 1)
                if live(0):
                    pool.wait_ge(s["w_scaled"], t + 1)
                    pool.tensor_tensor(part_of(t * 2 + 1, 1), raw(t * 2 + 1), part_of(t * 2 + 1, 0), ALU.subtract)\
                        .then_inc(s["w_lo_ok1"], 1)

            attention_steps(pool, step, 1, 2)

            def add_b2(t):
                pool.wait_ge(s["b2_rows_ok"], t + 1)
                pool.tensor_tensor(xs[:, t, :], b2_rows[t % 4], xs[:, t, :], ALU.add).then_inc(s["acc_ok"], 1)

            for t in range(T):
                add_b2(t)

            for n in range(2):
                pool.wait_ge(s[f"xd_out{n}"], 16 * T // 2)
            pool.wait_ge(s["zero_out"], 32)
            pool.wait_ge(s["rt"], RT_LIST)

            tiles = tile_count(pool)

            def moe(q, k, live):
                if live(3):
                    n = (k + 1) % 2
                    with filled(pool, tiles, q + 3):
                        wait(pool, f"gathered{n}", half_count(q + 1, n))
                        pool.tensor_copy(gcol[:, n, :], slot_row[:, at(q + 3)]).then_inc(s["gcol_ok"], 1)
                        wait(pool, "gcol_ok", q + 4)
                        wait_apart(pool, "xT_ps", q + 2)
                        pool.indirect_dma_start(xg[n], None, xd, bass.IndirectOffsetOnAxis(gcol[:, n, :], 0))\
                            .then_inc(s[f"gathered{n}"], 16)
                if live(-1):
                    n = (k + 1) % 2
                    if isinstance(q, int) and q == 1:
                        pool.wait_ge(s["acc_out"], 16 * B)
                    with filled(pool, tiles, q - 1):
                        wait(pool, "scattered", q * 16 - 16)
                        pool.tensor_copy(scol[:, n, :], slot_row[:, at(q - 1)]).then_inc(s["scol_ok"], 1)
                        wait(pool, "scol_ok", q)
                        wait_apart(pool, "y_ok", q)
                        pool.indirect_dma_start(acc, bass.IndirectOffsetOnAxis(scol[:, n, :], 0), y_sb[n], None,
                                                compute_op=ALU.add).then_inc(s["scattered"], 16)

            expert_steps(pool, moe, 3, 1)
            wait_apart(pool, "scattered", tiles * 16)

        @block.scalar
        def _(act):
            act.dma_start(gates[:, 0:1], g_xattn.rearrange("(o n) -> o n", o=1).to_broadcast([P, 1]))\
                .then_inc(s["small_in"], 16)
            act.dma_start(gates[:, 1:2], g_ffn.rearrange("(o n) -> o n", o=1).to_broadcast([P, 1]))\
                .then_inc(s["small_in"], 16)
            act.dma_start(b1_raw[:, :], b1.rearrange("e (c p) -> (e c) p", p=P)).then_inc(s["small_in"], 16)
            act.dma_start(gate_raw[:, :], gate_w).then_inc(s["small_in"], 16)
            act.dma_start(b2_sb[:, :], b2).then_inc(s["small_in"], 16)
            act.wait_ge(s["seg_ps"], 1)
            act.wait_ge(s["seg_flag"], 1)
            for g in range(4):
                act.activation(seg16[:, 512 * g:512 * g + 512], ps_ctxT[g], ACT.Copy).then_inc(s["seg_all"], 1)
            act.wait_ge(s["ps_wT"], 1)
            act.activation(WqT[:, :, :].rearrange("p k c -> p (k c)"), ps_sel[:, 0, :], ACT.Copy).then_inc(s["wT"], 1)
            act.activation(WkvT[:, 0, :], ps_sel[:, 1, :], ACT.Copy).then_inc(s["wT"], 1)
            act.activation(WkvT[:, 1, :], ps_sel[:, 2, :], ACT.Copy).then_inc(s["wT"], 1)
            act.activation(WoT[:, :, :].rearrange("p k c -> p (k c)"), ps_sel[:, 3, :], ACT.Copy).then_inc(s["wT"], 1)
            act.wait_ge(s["ps_small"], 1)
            act.activation(gateT[:, :, :].rearrange("p k c -> p (k c)"), ps_a[:, 0:KC * E], ACT.Copy)\
                .then_inc(s["small_T"], 1)
            act.activation(b1T[:, :], ps_a[:, 64:64 + E * FC], ACT.Copy).then_inc(s["small_T"], 1)
            act.wait_ge(s["small_in"], 80)
            act.activation(tanh_g[:, :], gates[:, :], ACT.Tanh).then_inc(s["gates_t"], 1)
            for b in range(B):
                act.wait_ge(s["ctxT_ps"], b + 1)
                act.activation(ctxT[b][:, :, :].rearrange("p k c -> p (k c)"), ps_ctxT[b][:, 0:256], ACT.Copy)\
                    .then_inc(s["ctxT_sb"], 1)
            for b in range(B + 1):
                if b < B:
                    act.wait_ge(s["kv_ps"], b + 1)
                    act.activation(kv3[:, 0, b, :], ps_sel[:, b, :], ACT.Copy).then_inc(s["kv_hi"], 1)
                if b > 0:
                    act.wait_ge(s["kv_r"], b)
                    act.activation(kv3[:, 1, b - 1, :], kv_rest[(b - 1) % 2], ACT.Copy).then_inc(s["kv_mid"], 1)

            general = flag(act)

            def chunk(n):
                act.wait_ge(s["g_ctxT_ps"], n + 1)
                act.activation(ctxT_g.rearrange("p k c -> p (k c)"), ps_t[:, 0:256], ACT.Copy).then_inc(s["g_ctxT"], 1)
                act.wait_ge(s["g_kv_ps"], n + 1)
                act.activation(kv_g, ps_sel[:, 0, :], ACT.Copy).then_inc(s["g_kv"], 1)

            with act.If(general > 0):
                with act.Fori(0, B * (CHUNKS + 1)) as n:
                    chunk(n)

            def step(t, k, live):
                if live(1):
                    act.wait_ge(s["xnT_ps"], t + 2)
                    wait(act, "q_ps", t + 1)
                    act.activation(xnT[:, :, :].rearrange("p k c -> p (k c)"), ps_t[:, 0:256], ACT.Copy)\
                        .then_inc(s["xnT_ok"], 1)
                if live(-1):
                    act.wait_ge(s["aT_ps"], t)
                    wait(act, "o_ps", t - 1)
                    act.activation(aT[:, :, :].rearrange("p k c -> p (k c)"), ps_a[:, 0:256], ACT.Copy)\
                        .then_inc(s["aT_ok"], 1)
                if live(0):
                    act.wait_ge(s[f"w_in{k}"], (t - k) * 4 + 16)
                    wait_apart(act, "w_lo_ok0", t)
                    act.activation(part_of(t * 2, 0), raw(t * 2), ACT.Copy, scale=W_SCALE).then_inc(s["w_hi_ok0"], 1)
                if live(-2):
                    act.wait_ge(s["x2T_ps"], t - 1)
                    wait(act, "logit_ps", t - 2)
                    act.activation(x2T[:, :, :].rearrange("p k c -> p (k c)"), ps_t[:, 256:512], ACT.Copy)\
                        .then_inc(s["x2T_ok"], 1)
                if live(0):
                    act.wait_ge(s["shifted"], t + 1)
                    act.activation(prob[:, k % 2, :, :].rearrange("p j h -> p (j h)"),
                                   score[:, k % 2, :, :].rearrange("p j h -> p (j h)"), ACT.Exp,
                                   scale=float(HD) ** -0.5).then_inc(s["exped"], 1)
                if live(1):
                    with act.If(general < 1):
                        wait(act, "aT_ps", t)
                        for j in range(WIN):
                            act.wait_ge(s["sel_ps"], t * WIN + (WIN + j + 1))
                            act.activation(sel[:, (k + 1) % 2, j, :], ps_sel[:, j, :], ACT.Copy)\
                                .then_inc(s["sel_ok"], 1)
                if live(-2):
                    act.wait_ge(s["logit_ps"], t - 1)
                    act.activation(tile_of(logit, t - 2), ps_a[:, 256:256 + E], ACT.Copy, scale=1.0 / X_SCALE)\
                        .then_inc(s["logit_ok"], 1)
                if live(0):
                    act.wait_ge(s[f"w_in{k}"], (t - k) * 4 + 16)
                    wait_apart(act, "w_lo_ok1", t)
                    act.activation(part_of(t * 2 + 1, 0), raw(t * 2 + 1), ACT.Copy, scale=W_SCALE)\
                        .then_inc(s["w_hi_ok1"], 1)
                    wait_apart(act, "w_hi_ok1", t + 1)
                    act.activation(raw(t * 2 + 1), raw(t * 2 + 1), ACT.Copy, scale=W_SCALE)\
                        .then_inc(s["w_scaled"], 1)

            attention_steps(act, step, 1, 2)

            act.wait_ge(s["rt"], RT_SHIFT)
            act.activation(r_ex[:, :, :], r_tmp[:, :, :], ACT.Exp).then_inc(s["rt_exp"], 1)
            act.activation(var2[:, :], half[:, 0:1], ACT.Silu).then_inc(s["unused"], 1)
            for g in range(4):
                act.wait_ge(s["combT_ps"], g + 1)
                act.activation(r_combT[:, 4 * g:4 * g + 4, :].rearrange("e t p -> e (t p)"), ps_sel[0:E, g, :],
                               ACT.Copy).then_inc(s["combT_ok"], 1)
            for t in range(T):
                act.wait_ge(s["b2_ps"], t + 1)
                wait(act, "acc_ok", t - 3)
                act.activation(b2_rows[t % 4], b2_bank[t % 4][:, 0:D], ACT.Copy).then_inc(s["b2_rows_ok"], 1)

            def moe(q, k, live):
                if live(0):
                    n = k % 2
                    with filled(act, tiles, q):
                        e = act.value_load(tile_e[0:1, at(q)], min_val=0, max_val=E - 1)
                        biases = b1T[:, bass.ds(e * FC, FC)]
                        wait(act, "hlo_ok", q * 2 - 2)
                        for c in range(FC):
                            if c % 4 == 0:
                                act.wait_ge(s["h_ps"], q * 2 + (c // 4 + 1))
                            act.activation(h32[n][:, c * P:c * P + P], ps_h[n][:, c * P:c * P + P], ACT.Silu,
                                           bias=biases[:, c:c + 1], scale=1.0 / (X_SCALE * W_SCALE))\
                                .then_inc(s["silu_ok"], 1)

            act.wait_ge(s["rt"], RT_LIST)
            tiles = tile_count(act)
            expert_steps(act, moe, 0, 0)

        @block.tensor
        def _(pe):
            pe.wait_ge(s["consts"], 8)
            pe.wait_ge(s["seg_cast"], 1)
            for g in range(4):
                mm = pe.matmul(ps_ctxT[g], ones16[0:1, :], seg16[0:1, 512 * g:512 * g + 512], start=True, stop=True)
            mm.then_inc(s["seg_ps"], 1)
            pe.wait_ge(s["wraw_in"], 48)
            for o in range(2):
                for c in range(KC):
                    pe.transpose(ps_sel[:, 0, c * D + o * P:c * D + o * P + P], wq_raw[:, o, c * P:c * P + P], ident[:, :])
                    pe.transpose(ps_sel[:, 3, c * D + o * P:c * D + o * P + P], wo_raw[:, o, c * P:c * P + P], ident[:, :])
            for o in range(4):
                for c in range(KC):
                    mm = pe.transpose(ps_sel[:, 1 + c, o * P:o * P + P], wkv_raw[:, o, c * P:c * P + P], ident[:, :])
            mm.then_inc(s["ps_wT"], 1)
            pe.wait_ge(s["small_in"], 80)
            pe.wait_ge(s["seg_all"], 4)
            for c in range(KC):
                pe.transpose(ps_a[:, c * E:c * E + E], gate_raw[:, c * P:c * P + P], ident[0:E, 0:E])
            pe.transpose(ps_a[:, 64:64 + E * FC], b1_raw[:, :], ident[0:E * FC, 0:E * FC]).then_inc(s["ps_small"], 1)
            pe.wait_ge(s["seg_f"], 1)
            pe.wait_ge(s["wT"], 4)
            pe.transpose(ps_sel[:, 3, 0:T], segr[:, :], ident[0:T, 0:T]).then_inc(s["segt_ps"], 1)
            pe.wait_ge(s["ctx_in"], 16)
            pe.wait_ge(s["small_T"], 2)
            for b in range(B):
                for c in range(KC):
                    mm = pe.transpose(ps_ctxT[b][:, P * c:P * c + P], ctx0[:, b, c * P:c * P + P], ident[:, :])
                mm.then_inc(s["ctxT_ps"], 1)
            for b in range(B):
                if b == 3:
                    pe.wait_ge(s["seg_cast"], 3)
                pe.wait_ge(s["ctxT_sb"], b + 1)
                for c in range(KC):
                    mm = pe.matmul(ps_sel[:, b, :], ctxT[b][:, c, :], WkvT[:, c, :], start=(c == 0), stop=(c == KC - 1))
                mm.then_inc(s["kv_ps"], 1)

            general = flag(pe)

            def chunk(n):
                pe.wait_ge(s["g_ctx"], n * 16 + 16)
                for c in range(KC):
                    mm = pe.transpose(ps_t[:, P * c:P * c + P], ctx_g[:, c * P:c * P + P], ident[:, :])
                mm.then_inc(s["g_ctxT_ps"], 1)
                pe.wait_ge(s["g_ctxT"], n + 1)
                for c in range(KC):
                    mm = pe.matmul(ps_sel[:, 0, :], ctxT_g[:, c, :], WkvT[:, c, :], start=(c == 0), stop=(c == KC - 1))
                mm.then_inc(s["g_kv_ps"], 1)

            with pe.If(general > 0):
                with pe.Fori(0, B * (CHUNKS + 1)) as n:
                    chunk(n)

            pe.wait_ge(s["kv_done"], B)

            def step(t, k, live):
                if live(1):
                    pe.wait_ge(s["xn_ok"], t + 2)
                    wait(pe, "xnT_ok", t + 1)
                    for c in range(KC):
                        mm = pe.transpose(ps_t[:, c * P:c * P + P], xn[:, c * P:c * P + P], ident[:, :])
                    mm.then_inc(s["xnT_ps"], 1)
                if live(-1):
                    pe.wait_ge(s["v_ok"], t)
                    wait(pe, "aT_ok", t - 1)
                    wait(pe, "logit_ok", t - 2)
                    for c in range(KC):
                        for j in range(WIN):
                            mm = pe.matmul(ps_a[:, c * P:c * P + P], sel[:, (k + 1) % 2, j, D + c * P:D + c * P + P],
                                           ident[:, :], start=(j == 0), stop=(j == WIN - 1))
                    mm.then_inc(s["aT_ps"], 1)
                if live(-2):
                    if live(1):
                        pe.wait_ge(s["xnT_ok"], t + 2)
                    pe.wait_ge(s["x2_ok"], t - 1)
                    for c in range(KC):
                        mm = pe.transpose(ps_t[:, 256 + c * P:256 + c * P + P], x2[:, c * P:c * P + P], ident[:, :])
                    mm.then_inc(s["x2T_ps"], 1)
                if live(-1):
                    pe.wait_ge(s["aT_ok"], t)
                    wait(pe, "x1_ok", t - 1)
                    for c in range(KC):
                        mm = pe.matmul(ps_o[:, 0:D], aT[:, c, :], WoT[:, c, :], start=(c == 0), stop=(c == KC - 1))
                    mm.then_inc(s["o_ps"], 1)
                if live(1):
                    with pe.If(general < 1):
                        pe.wait_ge(s["hot_ok"], t + 2)
                        for j in range(WIN):
                            wait(pe, "sel_ok", t * WIN + (j + 1))
                            for m in range(3):
                                if isinstance(t, int):
                                    rows = kv3[:, m, (t + 1) // TPB, :]
                                else:
                                    rows = kv3[:, m, bass.ds(pe_batch[0] + (1 if k == 3 else 0), 1), :]\
                                        .rearrange("p o c -> p (o c)")
                                mm = pe.matmul(ps_sel[:, j, :], onehot[:, (k + 1) % 2, j, :], rows,
                                               start=(m == 0), stop=(m == 2))
                            mm.then_inc(s["sel_ps"], 1)
                if live(-2):
                    pe.wait_ge(s["x2T_ok"], t - 1)
                    if live(-1):
                        pe.wait_ge(s["aT_ok"], t)
                    for c in range(KC):
                        mm = pe.matmul(ps_a[:, 256:256 + E], x2T[:, c, :], gateT[:, c, :],
                                       start=(c == 0), stop=(c == KC - 1))
                    mm.then_inc(s["logit_ps"], 1)
                if live(1):
                    pe.wait_ge(s["xnT_ok"], t + 2)
                    wait(pe, "kprod", t + 1)
                    for c in range(KC):
                        mm = pe.matmul(ps_q[:, 0:D], xnT[:, c, :], WqT[:, c, :], start=(c == 0), stop=(c == KC - 1))
                    mm.then_inc(s["q_ps"], 1)

            pe_batch = [None]

            def attention_pe():
                def fixed(t):
                    step(t, t % 4, lambda d: 0 <= t + d < T)
                for t in range(-1, 4):
                    fixed(t)
                with pe.Fori(1, 3) as b:
                    pe_batch[0] = b
                    for k in range(4):
                        step(b * 4 + k, k, lambda d: True)
                for t in range(12, T + 2):
                    fixed(t)

            attention_pe()

            pe.wait_ge(s["rt"], RT_PAIRS)
            m16 = r_m16[:, :, :].rearrange("p t e -> p (t e)")
            pe.matmul(ps_q[:, 0:P], before[:, :], m16, start=True, stop=True)
            pe.matmul(ps_q[:, P:2 * P], ones16[:, :], m16, start=True, stop=True).then_inc(s["rt_ps"], 1)
            pe.wait_ge(s["rt"], RT_COMB)
            for t in range(T):
                mm = pe.transpose(ps_sel[0:E, t // 4, (t % 4) * P:(t % 4) * P + P], r_comb[:, t, :], ident[:, :])
                if t % 4 == 3:
                    mm.then_inc(s["combT_ps"], 1)

            def b2_part(t):
                if t < 4:
                    pe.wait_ge(s["combT_ok"], 4)
                wait(pe, "b2_rows_ok", t - 3)
                pe.matmul(b2_bank[t % 4][:, 0:D], r_combT[:, t, :], b2_sb[:, :], start=True, stop=True)\
                    .then_inc(s["b2_ps"], 1)

            for t in range(T):
                b2_part(t)
            for n in range(2 * T):
                if n % T == 0:
                    pe.wait_ge(s["rt"], RT_HOT + n // T)
                mm = pe.matmul(ps_o[:, 0:3 * NT], row_hot[:, n, :],
                               col_val[:, n, :, :].rearrange("p i q -> p (i q)"),
                               start=(n == 0), stop=(n == 2 * T - 1))
            mm.then_inc(s["list_ps"], 1)
            pe.wait_ge(s["w_lo_ok0"], T)
            pe.wait_ge(s["w_lo_ok1"], T)
            pe.wait_ge(s["b2_rows_ok"], T)
            pe.wait_ge(s["rt"], RT_LIST)
            tiles = tile_count(pe)
            expert_of = [pe.alloc_register(f"expert_{n}") for n in range(4)]
            expert_before = {n: pe.alloc_register(f"expert_before_{n}") for n in (3, 0)}

            w_bytes = w_parts[:, :, :, :].rearrange("p u a c -> p (u a c)").bitcast(U8)

            def expert_byte(register):
                return pe.snap(pe.snap(register, min_val=0, max_val=E - 1) * (4 * 2 * UC * 2))

            def weights_at(first, unit, part, column, n):
                return w_bytes[:, bass.ds(first + (((unit * 2 + part) * UC + column) * 2), n * 2)].bitcast(F16)

            def up_chunk(q, n, c, first):
                products = []
                for kc in range(KC):
                    hi = weights_at(first, kc, 0, c * P, P)
                    lo = weights_at(first, kc, 1, c * P, P)
                    products += [(hi, xT[n][:, kc, :]), (hi, xT[n][:, KC + kc, :]), (lo, xT[n][:, kc, :])]
                for i, (w, xx) in enumerate(products):
                    mm = pe.matmul(ps_h[n][:, c * P:c * P + P], w, xx, start=(i == 0), stop=(i == len(products) - 1))
                if c % 4 == 3:
                    mm.then_inc(s["h_ps"], 1)

            def inputs_ready(q):
                wait_apart(pe, "xT_ok", q + 2)

            def down_chunk(q, n, c, first):
                both = weights_at(first, KC + c // 4, 0, c % 4 * D, 2 * UC).rearrange("p (a c) -> p a c", a=2)[:, :, 0:D]
                rhi = weights_at(first, KC + c // 4, 0, c % 4 * D, D)
                hi, lo = h_hi[n][:, c * P:c * P + P], h_lo[n][:, c * P:c * P + P]
                sides = ps_y[n].rearrange("p (a c) -> p a c", a=2)
                if c < FC - 1:
                    pe.matmul(sides, hi, both, start=(c == 0), stop=False)
                    pe.matmul(ps_y[n][:, 0:D], lo, rhi, start=False, stop=False)
                else:
                    pe.matmul(ps_y[n][:, 0:D], lo, rhi, start=False, stop=False)
                    pe.matmul(sides, hi, both, start=False, stop=True).then_inc(s["y_ps"], 1)

            def turn(q, n):
                wait(pe, f"gathered{n}", half_count(q, n))
                for h in range(4):
                    mm = pe.transpose(ps_x16[:, h * P:h * P + P], xg[n][:, h * P:h * P + P], ident16[:, :])
                mm.then_inc(s["xT_ps"], 1)

            def moe(q, k, live):
                n = (k + 1) % 2
                up, down = expert_of[(k + 1) % 4], expert_before.get((k - 1) % 4, expert_of[(k - 1) % 4])
                if isinstance(q, int) and q == -1:
                    pe.reg_load(up, tile_e[0:1, 0:1])
                if isinstance(q, int) and q + 1 >= FULL:
                    if live(1):
                        with filled(pe, tiles, q + 1):
                            first = expert_byte(up)
                            inputs_ready(q)
                            for c in range(FC):
                                up_chunk(q + 1, n, c, first)
                    if live(2):
                        with filled(pe, tiles, q + 2):
                            turn(q + 2, n ^ 1)
                    with filled(pe, tiles, q - 1):
                        first = expert_byte(down)
                        pe.wait_ge(s["hlo_ok"], q * 2)
                        for c in range(FC):
                            down_chunk(q - 1, n, c, first)
                else:
                    if live(1):
                        up_first = expert_byte(up)
                        inputs_ready(q)
                    if live(-1):
                        down_first = expert_byte(down)
                    for c in range(FC):
                        if live(1):
                            up_chunk(q + 1, n, c, up_first)
                        if live(-1):
                            down_chunk(q - 1, n, c, down_first)
                        if live(2) and c == FC // 2:
                            with filled(pe, tiles, q + 2):
                                turn(q + 2, n ^ 1)
                if k == 3:
                    for m in range(2):
                        if live(m):
                            pe.reg_mov(expert_before[(k + m) % 4], expert_of[(k + m) % 4])
                    if live(2):
                        count = min(4, NT - 2 - q) if isinstance(q, int) else 4
                        some = slice(q + 2, q + 2 + count) if isinstance(q, int) else bass.ds(q + 2, count)
                        pe.reg_load([expert_of[(1 + m) % 4] for m in range(count)], tile_e[0:1, some])

            expert_steps(pe, moe, 2, 1)

        @block.vector
        def _(dve):
            v = nc.vector
            dve.wait_ge(s["consts"], 13)
            v.tensor_copy(ident16[:, :], ident[:, :]).then_inc(s["cast_consts"], 1)
            v.tensor_copy(iota[:, :], iota_i[:, :]).then_inc(s["cast_consts"], 1)
            v.tensor_copy(part[:, :], part_i[:, :]).then_inc(s["cast_consts"], 1)
            v.tensor_copy(tok16[:, :], tok_i[:, :]).then_inc(s["cast_consts"], 1)
            v.tensor_copy(iota16[:, :], iota_i[:, :]).then_inc(s["cast_consts"], 1)
            dve.wait_ge(s["cast_consts"], 5)
            v.tensor_scalar(pad_row[:, :], part[:, 0:1], float(N_TOK + 1), None, ALU.add).then_inc(s["cast_consts"], 1)
            dve.wait_ge(s["seg_in"], 32)
            v.tensor_copy(segr[:, :], segr_i[:, :]).then_inc(s["seg_f"], 1)
            v.tensor_scalar(seg16[0:1, :], seg_i, 2047.0, -8.0, ALU.min, ALU.max).then_inc(s["seg_cast"], 1)
            dve.wait_ge(s["seg_cast"], 1)
            v.tensor_reduce(seg_max[:, :], seg16[0:1, :], AX_X, ALU.max).then_inc(s["seg_cast"], 1)
            dve.wait_ge(s["seg_cast"], 2)
            v.tensor_scalar(general_i[:, :], seg_max[:, :], float(P), None, ALU.is_ge).then_inc(s["seg_flag"], 1)
            for b in range(B):
                dve.wait_ge(s[f"x_in{b}"], 16)
                for t in range(TPB * b, TPB * b + TPB):
                    v.bn_stats(st1[:, t, :], xs[:, t, :]).then_inc(s["stats1"], 1)
            for t in range(T):
                dve.wait_ge(s["stats1"], t + 1)
                v.bn_aggr(mv1[:, t, :], st1[:, t, :]).then_inc(s["aggr1"], 1)
            dve.wait_ge(s["segt_ps"], 1)
            v.tensor_copy(segt[:, :], ps_sel[:, 3, 0:T]).then_inc(s["seg_cast"], 1)
            dve.wait_ge(s["seg_cast"], 3)
            for j in range(WIN):
                v.tensor_scalar(mask[:, :, j], segt[:, :], float(j), MASKED, ALU.is_lt, ALU.mult)
                v.tensor_scalar(win_f[:, :, j], segt[:, :], float(-j), 0.0, ALU.add, ALU.max).then_inc(s["seg_cast"], 1)
            dve.wait_ge(s["seg_cast"], 3 + WIN)
            for b in range(B):
                last = v.tensor_scalar(win_i[:, TPB * b:TPB * b + TPB, :], win_f[:, TPB * b:TPB * b + TPB, :],
                                       float(CTX - 1), float(b * CTX), ALU.min, ALU.add)
            last.then_inc(s["setup"], 1)

            for b in range(B + 1):
                if b < B:
                    dve.wait_ge(s["kv_hi"], b + 1)
                    wait(dve, "kv_done", b - 1)
                    v.tensor_tensor(kv_rest[b % 2], ps_sel[:, b, :], kv3[:, 0, b, :], ALU.subtract)\
                        .then_inc(s["kv_r"], 1)
                if b > 0:
                    dve.wait_ge(s["kv_mid"], b)
                    v.tensor_tensor(kv3[:, 2, b - 1, :], kv_rest[(b - 1) % 2], kv3[:, 1, b - 1, :], ALU.subtract)\
                        .then_inc(s["kv_done"], 1)

            dve.wait_ge(s["rstd1_ok"], 1)
            dve.wait_ge(s["gates_t"], 1)
            dve.wait_ge(s["seg_all"], 4)
            dve.wait_ge(s["zero_out"], 32)

            general = flag(dve)

            def step(t, k, live):
                c, n = k % 2, (k + 1) % 2
                if live(0):
                    keys = sel[:, c, :, 0:D]
                    dve.wait_ge(s["q_ps"], t + 1)
                    dve.wait_ge(s["sel_ok"], t * WIN + WIN)
                    v.tensor_tensor(keys, keys, spread_mid(ps_q[:, 0:D], WIN), ALU.mult).then_inc(s["kprod"], 1)
                if live(-2):
                    dve.wait_ge(s["rstd2_ok"], t - 1)
                    wait(dve, "x2T_ps", t - 2)
                    wait(dve, "xsplit_ok", t - 2)
                    row = tile_of(xs, t - 2)
                    v.tensor_scalar(x2[:, :], row, mv2[:, c, 0:1], rstd2[:, c, :], ALU.subtract, ALU.mult)\
                        .then_inc(s["x2_ok"], 1)
                if live(0):
                    dve.wait_ge(s["kprod"], t + 1)
                    v.tensor_reduce(score[:, c, :, :], keys.rearrange("p j (h d) -> p j h d", d=HD), AX_X, ALU.add)\
                        .then_inc(s["scored"], 1)
                if live(-2):
                    dve.wait_ge(s["x2_ok"], t - 1)
                    wait(dve, f"xd_out{c}", half_count(t - 4, c))
                    v.tensor_copy(xsplit[:, c, 0:D], x2[:, :]).then_inc(s["x2hi_ok"], 1)
                if live(0):
                    dve.wait_ge(s["scored"], t + 1)
                    m = tile_of(mask, t).rearrange("p (j o) -> p j o", o=1).to_broadcast([P, WIN, HEADS])
                    v.tensor_tensor(score[:, c, :, :], score[:, c, :, :], m, ALU.add).then_inc(s["masked"], 1)
                if live(2):
                    wait(dve, "xnT_ps", t + 2)
                    v.tensor_scalar(xn[:, :], tile_of(xs, t + 2), mv1[:, at(t + 2), 0], rstd1[:, at(t + 2)],
                                    ALU.subtract, ALU.mult).then_inc(s["xn_ok"], 1)
                if live(0):
                    dve.wait_ge(s["masked"], t + 1)
                    v.tensor_reduce(top[:, :], score[:, c, :, :].rearrange("p j h -> p h j"), AX_X, ALU.max)\
                        .then_inc(s["topped"], 1)
                if live(0):
                    dve.wait_ge(s["topped"], t + 1)
                    v.tensor_tensor(score[:, c, :, :], score[:, c, :, :], spread_mid(top[:, :], WIN), ALU.subtract)\
                        .then_inc(s["shifted"], 1)
                if live(2):
                    with dve.If(general < 1):
                        wait(dve, "sel_ps", t * WIN + WIN)
                        for j in range(WIN):
                            if isinstance(t, int):
                                sg = seg16[:, (t + 2) * P:(t + 3) * P]
                            else:
                                sg = seg16[:, bass.ds((t + 2) * P, P)]
                            last = v.tensor_scalar(onehot[:, c, j, :], sg, float(j), part[:, j:j + 1],
                                                   ALU.max, ALU.is_equal)
                        last.then_inc(s["hot_ok"], 1)
                if live(0):
                    dve.wait_ge(s["exped"], t + 1)
                    v.tensor_reduce(den[:, :], prob[:, c, :, :].rearrange("p j h -> p h j"), AX_X, ALU.add)\
                        .then_inc(s["summed"], 1)
                if live(0):
                    dve.wait_ge(s["summed"], t + 1)
                    v.reciprocal(rden[:, :], den[:, :]).then_inc(s["inverted"], 1)
                    dve.wait_ge(s["inverted"], t + 1)
                    v.tensor_tensor(prob[:, c, :, :], prob[:, c, :, :], spread_mid(rden[:, :], WIN), ALU.mult)\
                        .then_inc(s["prob_ok"], 1)
                if live(-1):
                    dve.wait_ge(s["o_ps"], t)
                    row = tile_of(xs, t - 1)
                    v.scalar_tensor_tensor(out=row, in0=ps_o[:, 0:D], scalar=tanh_g[:, 0:1], in1=row,
                                           op0=ALU.mult, op1=ALU.add).then_inc(s["x1_ok"], 1)
                if live(0):
                    dve.wait_ge(s["w_hi_ok0"], t + 1)
                    v.scalar_tensor_tensor(out=part_of(t * 2, 1), in0=raw(t * 2), scalar=W_SCALE,
                                           in1=part_of(t * 2, 0), op0=ALU.mult, op1=ALU.subtract)\
                        .then_inc(s["w_lo_ok0"], 1)
                if live(-1):
                    wait_apart(dve, "x1_ok", t)
                    v.bn_stats(st2[:, :], tile_of(xs, t - 1)).then_inc(s["stats2"], 1)
                if live(-1):
                    wait_apart(dve, "stats2", t)
                    v.bn_aggr(mv2[:, n, :], st2[:, :]).then_inc(s["aggr2"], 1)

            attention_steps(dve, step, 2, 2)

            done = [0]

            def link(ins):
                done[0] += 1
                ins.then_inc(s["rt"], 1)
                dve.wait_ge(s["rt"], done[0])

            def by_expert(ap):
                return ap.rearrange("p (t o) -> p t o", o=1).to_broadcast([P, T, E])

            dve.wait_ge(s["logit_ok"], T)
            dve.wait_ge(s["xsplit_ok"], T)
            link(v.tensor_reduce(r_mx[:, :], logit[:, :, :], AX_X, ALU.max))
            link(v.tensor_tensor(r_tmp[:, :, :], logit[:, :, :], by_expert(r_mx[:, :]), ALU.subtract))
            assert done[0] == RT_SHIFT
            dve.wait_ge(s["rt_exp"], 1)
            link(v.tensor_reduce(r_sum[:, :], r_ex[:, :, :], AX_X, ALU.add))
            link(v.reciprocal(r_rs[:, :], r_sum[:, :]))
            link(v.tensor_tensor(r_p[:, :, :], r_ex[:, :, :], by_expert(r_rs[:, :]), ALU.mult))
            for t in range(T):
                ins = v.max(r_m8[:, t, :], r_p[:, t, :])
            link(ins)
            for t in range(T):
                ins = v.max_index(r_i8[:, t, :], r_m8[:, t, :], r_p[:, t, :])
            link(ins)
            link(v.tensor_copy(r_i2[:, :, :], r_i8[:, :, 0:2]))
            experts = spread_mid(iota[:, 0:E], T)
            for a in range(2):
                ins = v.tensor_tensor(r_oh[:, a, :, :], r_i2[:, :, a:a + 1].to_broadcast([P, T, E]), experts,
                                      ALU.is_equal)
            link(ins)
            link(v.tensor_tensor(r_m16[:, :, :], r_oh[:, 0, :, :], r_oh[:, 1, :, :], ALU.add))
            assert done[0] == RT_PAIRS
            for a in range(2):
                ins = v.tensor_scalar(r_w[:, a, :], r_m8[:, :, a], tanh_g[:, 1:2], None, ALU.mult)
            link(ins)
            for a in range(2):
                ins = v.tensor_tensor((r_ex, r_tmp)[a][:, :, :], r_oh[:, a, :, :], by_expert(r_w[:, a, :]), ALU.mult)
            link(ins)
            link(v.tensor_tensor(r_comb[:, :, :], r_ex[:, :, :], r_tmp[:, :, :], ALU.add))
            assert done[0] == RT_COMB
            w_all = r_w[:, :, :].rearrange("p a t -> p (a t)")
            link(v.tensor_scalar(w_all, w_all, W_SCALE, None, ALU.mult))
            link(v.tensor_copy(r_pair[:, 2, :], w_all))
            link(v.tensor_tensor(r_pair[:, 3, :], w_all, r_pair[:, 2, :], ALU.subtract))
            dve.wait_ge(s["rt_ps"], 1)
            totals = ps_q[:, P:2 * P].rearrange("p (t e) -> p e t", e=E)
            link(v.tensor_copy(r_tot[:, :, :], totals))
            link(v.tensor_tensor_scan(r_inc[:, :, :].rearrange("p e t -> p (e t)"),
                                      r_go[:, :, :].rearrange("p e t -> p (e t)"),
                                      r_tot[:, :, :].rearrange("p e t -> p (e t)"), 0.0, ALU.mult, ALU.add))
            link(v.tensor_tensor(r_exc[:, :, :], r_inc[:, :, :], r_tot[:, :, :], ALU.subtract))
            link(v.tensor_scalar(r_ni[:, :], r_inc[:, :, T - 1], float(P - 1), None, ALU.add))
            link(v.tensor_scalar(r_ti[:, :], r_ni[:, :], 7, None, ALU.logical_shift_right))
            link(v.tensor_copy(r_tf[:, :], r_ti[:, :]))
            link(v.tensor_tensor_scan(r_end[:, :], r_one[:, :], r_tf[:, :], 0.0, ALU.mult, ALU.add))
            link(v.tensor_tensor(r_start[:, :], r_end[:, :], r_tf[:, :], ALU.subtract))
            link(v.tensor_scalar(r_start[:, :], r_start[:, :], float(P), None, ALU.mult))
            link(v.tensor_tensor(r_base[:, :, :], ps_q[:, 0:P].rearrange("p (t e) -> p t e", e=E),
                                 r_exc[:, :, :].rearrange("p e t -> p t e"), ALU.add))
            link(v.tensor_tensor(r_base[:, :, :], r_base[:, :, :], spread_mid(r_start[:, :], T), ALU.add))
            for a in range(2):
                link(v.tensor_tensor(r_tmp[:, :, :], r_oh[:, a, :, :], r_base[:, :, :], ALU.mult))
                link(v.tensor_reduce(r_slot[:, a, :], r_tmp[:, :, :], AX_X, ALU.add))
            link(v.tensor_copy(r_si[:, :, :], r_slot[:, :, :]))
            v.tensor_scalar(r_qi[:, :, :], r_si[:, :, :], 7, None, ALU.logical_shift_right)
            link(v.tensor_scalar(r_ri[:, :, :], r_si[:, :, :], P - 1, None, ALU.bitwise_and))
            v.tensor_copy(r_pair[:, 0, :], r_qi[:, :, :].rearrange("p a t -> p (a t)"))
            link(v.tensor_copy(r_pair[:, 1, :], r_ri[:, :, :].rearrange("p a t -> p (a t)")))
            dve.wait_ge(s["aT_ps"], T)

            def over_tiles(value, n):
                return value.rearrange("p (n o) -> p n o", o=1).to_broadcast([P, value.shape[1], n])

            link(v.tensor_tensor(col_val[:, :, 0, :], spread_mid(iota16[:, 0:NT], 2 * T),
                                 over_tiles(r_pair[:, 0, :], NT), ALU.is_equal))
            v.tensor_tensor(col_val[:, :, 1, :], col_val[:, :, 0, :], over_tiles(r_pair[:, 2, :], NT), ALU.mult)
            link(v.tensor_tensor(col_val[:, :, 2, :], col_val[:, :, 0, :], over_tiles(r_pair[:, 3, :], NT), ALU.mult))
            for a in range(2):
                half_val = col_val[:, T * a:T * a + T, 0, :]
                v.tensor_tensor(half_val, half_val, over_tiles(tok16[:, :], NT), ALU.mult)
            for a in range(2):
                link(v.tensor_tensor(row_hot[:, T * a:T * a + T, :], spread_mid(iota16[:, :], T),
                                     over_tiles(r_pair[:, 1, T * a:T * a + T], P), ALU.is_equal))
                assert done[0] == RT_HOT + a
            tiles = iota[:, 0:NT].rearrange("p (q o) -> p q o", o=1).to_broadcast([P, NT, E])
            for n in range(2):
                dve.wait_ge(s[f"xd_out{n}"], 16 * T // 2)
            link(v.tensor_tensor(l_cmp[:, :, :], spread_mid(r_end[:, :], NT), tiles, ALU.is_le))
            link(v.tensor_reduce(l_e[:, :], l_cmp[:, :, :], AX_X, ALU.add))
            v.tensor_copy(tiles_i[:, :], r_end[:, E - 1:E])
            link(v.tensor_scalar(tile_e[:, :], l_e[:, :], float(E - 1), None, ALU.min))
            dve.wait_ge(s["list_ps"], 1)
            link(v.tensor_scalar(l_empty[:, :], ps_o[:, 0:NT], 0.5, pad_row[:, 0:1], ALU.is_lt, ALU.mult))
            link(v.tensor_scalar(l_idx[:, :], ps_o[:, 0:NT], -1.0, None, ALU.add))
            v.tensor_scalar(l_w[:, :], ps_o[:, 2 * NT:3 * NT], W_UNSCALE, None, ALU.mult)
            link(v.tensor_tensor(slot_row[:, :], l_idx[:, :], l_empty[:, :], ALU.add))
            link(v.scalar_tensor_tensor(out=slot_w[:, :], in0=ps_o[:, NT:2 * NT], scalar=W_UNSCALE,
                                        in1=l_w[:, :], op0=ALU.mult, op1=ALU.add))
            assert done[0] == RT_LIST
            tiles = tile_count(dve)

            def moe(q, k, live):
                n, m = k % 2, (k + 1) % 2
                if live(0):
                    with filled(dve, tiles, q):
                        for h in range(2):
                            cols = slice(512 * h, 512 * h + 512)
                            dve.wait_ge(s["silu_ok"], q * FC + 4 * (h + 1))
                            wait(dve, "y_ps", q - 1)
                            v.tensor_scalar(h_hi[n][:, cols], h32[n][:, cols], H_SCALE, None, ALU.mult)\
                                .then_inc(s["hhi_ok"], 1)
                            dve.wait_ge(s["hhi_ok"], q * 2 + (h + 1))
                            v.scalar_tensor_tensor(out=h_lo[n][:, cols], in0=h32[n][:, cols], scalar=H_SCALE,
                                                   in1=h_hi[n][:, cols], op0=ALU.mult, op1=ALU.subtract)\
                                .then_inc(s["hlo_ok"], 1)
                if live(2):
                    with filled(dve, tiles, q + 2):
                        dve.wait_ge(s["xT_ps"], q + 3)
                        wait(dve, "h_ps", q * 2 + 2)
                        v.tensor_copy(xT[n].rearrange("p a c -> p (a c)"), ps_x16[:, 0:512]).then_inc(s["xT_ok"], 1)
                if live(-1):
                    with filled(dve, tiles, q - 1):
                        dve.wait_ge(s["y_ps"], q)
                        wait(dve, "scattered", q * 16 - 32)
                        v.tensor_scalar(y_low[m], ps_y[m][:, D:2 * D], slot_w[:, at(q - 1)], None, ALU.mult)\
                            .then_inc(s["y_low_ok"], 1)
                        wait_apart(dve, "y_low_ok", q)
                        v.scalar_tensor_tensor(out=y_sb[m], in0=ps_y[m][:, 0:D], scalar=slot_w[:, at(q - 1)],
                                               in1=y_low[m], op0=ALU.mult, op1=ALU.add).then_inc(s["y_ok"], 1)

            expert_steps(dve, moe, 2, 1)


RT_SHIFT, RT_PAIRS, RT_COMB, RT_HOT, RT_LIST = 2, 10, 13, 37, 45

_INS = ["x", "ctx_1024", "itok_BxS_0_511", "g_xattn", "g_ffn", "L0_xattn_Wq", "L0_xattn_Wkv", "L0_xattn_Wo",
        "L0_ffn_gate_w", "L0_ffn_w1", "L0_ffn_b1", "L0_ffn_w2", "L0_ffn_b2"]


def kernel(**inputs):
    import numpy as _np
    import concourse.bacc as _bacc
    from concourse import mybir as _mybir
    from concourse.bass_utils import run_bass_kernel_spmd as _run

    nc = _bacc.Bacc("TRN2", target_bir_lowering=False, num_devices=1)
    arrays, args = {}, []
    for name in _INS:
        a = _np.ascontiguousarray(inputs[name])
        arrays[f"in_{name}"] = a
        args.append(nc.dram_tensor(f"in_{name}", a.shape, _mybir.dt.from_np(a.dtype), kind="ExternalInput").ap())
    shape = inputs["x"].shape
    args.append(nc.dram_tensor("out_0", shape, _mybir.dt.float32, kind="ExternalOutput").ap())
    flamingo_layer(nc, *args)
    r = _run(nc, [arrays], core_ids=[0])
    return r.results[0]["out_0"]
```
